# Optimizing a Trainium2 kernel written in Bass

```python
import numpy as np
import jax
import jax.numpy as jnp

def _softmax(x, axis=-1):
    return jax.nn.softmax(x, axis=axis)

def _gelu(x):
    return jax.nn.gelu(x, approximate=True)

def _silu(x):
    return jax.nn.silu(x)

def _sigmoid(x):
    return jax.nn.sigmoid(x)

def _layernorm(x, axis=-1, eps=1e-05):
    m = jnp.mean(x, axis=axis, keepdims=True)
    v = jnp.var(x, axis=axis, keepdims=True)
    return (x - m) / jnp.sqrt(v + eps)

def _scatter_add(tgt, idx, src, axis=0):
    return tgt.at[idx].add(src)

def _segment_sum(src, seg, n):
    return jax.ops.segment_sum(src, seg, n)
kernel_name = 'mk_adaln_d1_jaxref_r8_5782fc'

def setup_inputs(seed: int=0):
    np.random.seed(seed)
    _w = jnp.asarray

    def _L0_attn_setup():
        import jax, jax.numpy as jnp
        import numpy as np
        EMBED_DIM = 256
        NUM_HEADS = 16
        HEAD_DIM = EMBED_DIM // NUM_HEADS
        WINDOW = 64
        CHUNK = WINDOW
        SCALE = 1.0 / float(np.sqrt(HEAD_DIM))

        def _sliding_window_attention(q, k, v):
            B, H, S, D = q.shape
            C = CHUNK
            nc = S // C
            qc = q.reshape(B, H, nc, C, D)
            kp = jnp.pad(k, ((0, 0), (0, 0), (C, 0), (0, 0))).reshape(B, H, nc + 1, C, D)
            vp = jnp.pad(v, ((0, 0), (0, 0), (C, 0), (0, 0))).reshape(B, H, nc + 1, C, D)
            kc = jnp.concatenate([kp[:, :, :-1], kp[:, :, 1:]], axis=-2)
            vc = jnp.concatenate([vp[:, :, :-1], vp[:, :, 1:]], axis=-2)
            qa = jnp.arange(C)
            ka = jnp.arange(2 * C)
            diff = C + qa[:, None] - ka[None, :]
            base = (diff >= 0) & (diff <= WINDOW)
            kv_pos = (jnp.arange(nc)[:, None] - 1) * C + ka[None, :]
            mask = base[None, :, :] & (kv_pos >= 0)[:, None, :]
            scores = jnp.einsum('bhncd,bhnkd->bhnck', qc, kc) * SCALE
            scores = jnp.where(mask[None, None], scores, -jnp.inf)
            attn = jax.nn.softmax(scores, axis=-1)
            out = jnp.einsum('bhnck,bhnkd->bhncd', attn, vc)
            return out.reshape(B, H, S, D)
        key = jax.random.key(seed)
        k1, k2, k3 = jax.random.split(key, 3)
        B, S, E = (2, 512, EMBED_DIM)
        x = jax.random.normal(k1, (B, S, E), dtype=jnp.float32)
        w_qkv = jax.random.normal(k2, (3 * E, E), dtype=jnp.float32) * (1.0 / np.sqrt(E))
        w_out = jax.random.normal(k3, (E, E), dtype=jnp.float32) * (1.0 / np.sqrt(E))
        return {'x': x, 'w_qkv': w_qkv, 'w_out': w_out}
    _L0_attn_in = _L0_attn_setup()

    def _L0_ffn_setup():
        import jax, jax.numpy as jnp
        import numpy as np
        from jax import lax
        H = 256
        I = 176
        E = 16
        K = 4
        ISH = 2 * I
        B, S = (4, 256)

        def _router(xf, rg_w, ru_w, extra_scale, extra_bias):
            g = xf @ rg_w.T
            u = xf @ ru_w.T
            scores = jnp.abs(u * jax.nn.silu(g))
            probs = jax.nn.softmax(scores.astype(jnp.float32), axis=-1)
            biased = probs + extra_bias[None, :]
            _, idx = lax.top_k(biased, K)
            orig = 1.0 + probs * extra_scale[None, :]
            w = jnp.take_along_axis(orig, idx, axis=1).astype(xf.dtype)
            return (w, idx)
        key = jax.random.key(seed)
        ks = jax.random.split(key, 12)
        sc = 0.02
        return {'x': jax.random.normal(ks[0], (B, S, H), dtype=jnp.float32), 'rg_w': jax.random.normal(ks[1], (E, H), dtype=jnp.float32) * sc, 'ru_w': jax.random.normal(ks[2], (E, H), dtype=jnp.float32) * sc, 'extra_scale': jnp.zeros((E,), dtype=jnp.float32), 'extra_bias': jnp.zeros((E,), dtype=jnp.float32), 'Wg': jax.random.normal(ks[3], (E, I, H), dtype=jnp.float32) * sc, 'Wu': jax.random.normal(ks[4], (E, I, H), dtype=jnp.float32) * sc, 'Wd': jax.random.normal(ks[5], (E, H, I), dtype=jnp.float32) * sc, 'Sg': jax.random.normal(ks[6], (ISH, H), dtype=jnp.float32) * sc, 'Su': jax.random.normal(ks[7], (ISH, H), dtype=jnp.float32) * sc, 'Sd': jax.random.normal(ks[8], (H, ISH), dtype=jnp.float32) * sc}
    _L0_ffn_in = _L0_ffn_setup()
    _L0_c = _w((lambda *s: np.random.randn(*s).astype(np.float32) * 0.05)(1, 256))
    _L0_wmod = _w((lambda *s: np.random.randn(*s).astype(np.float32) * 0.05)(256, 6 * 256) * 256 ** (-0.5))
    _d = {'L0_attn_x': _L0_attn_in['x'], 'L0_attn_w_qkv': _L0_attn_in['w_qkv'], 'L0_attn_w_out': _L0_attn_in['w_out'], 'L0_ffn_rg_w': _L0_ffn_in['rg_w'], 'L0_ffn_ru_w': _L0_ffn_in['ru_w'], 'L0_ffn_extra_scale': _L0_ffn_in['extra_scale'], 'L0_ffn_extra_bias': _L0_ffn_in['extra_bias'], 'L0_ffn_Wg': _L0_ffn_in['Wg'], 'L0_ffn_Wu': _L0_ffn_in['Wu'], 'L0_ffn_Wd': _L0_ffn_in['Wd'], 'L0_ffn_Sg': _L0_ffn_in['Sg'], 'L0_ffn_Su': _L0_ffn_in['Su'], 'L0_ffn_Sd': _L0_ffn_in['Sd'], 'L0_c': _L0_c, 'L0_wmod': _L0_wmod}
    _x0 = _d['L0_attn_x']
    _d['L0_attn_x'] = jax.random.normal(jax.random.fold_in(jax.random.key(seed), 1), (1, 2048, 256), dtype=_x0.dtype)
    del _x0
    return _d

def reference(L0_attn_x, L0_attn_w_qkv, L0_attn_w_out, L0_ffn_rg_w, L0_ffn_ru_w, L0_ffn_extra_scale, L0_ffn_extra_bias, L0_ffn_Wg, L0_ffn_Wu, L0_ffn_Wd, L0_ffn_Sg, L0_ffn_Su, L0_ffn_Sd, L0_c, L0_wmod):

    def _L0_attn_ref(x, w_qkv, w_out):
        import jax, jax.numpy as jnp
        import numpy as np
        EMBED_DIM = 256
        NUM_HEADS = 16
        HEAD_DIM = EMBED_DIM // NUM_HEADS
        WINDOW = 64
        CHUNK = WINDOW
        SCALE = 1.0 / float(np.sqrt(HEAD_DIM))

        def _sliding_window_attention(q, k, v):
            B, H, S, D = q.shape
            C = CHUNK
            nc = S // C
            qc = q.reshape(B, H, nc, C, D)
            kp = jnp.pad(k, ((0, 0), (0, 0), (C, 0), (0, 0))).reshape(B, H, nc + 1, C, D)
            vp = jnp.pad(v, ((0, 0), (0, 0), (C, 0), (0, 0))).reshape(B, H, nc + 1, C, D)
            kc = jnp.concatenate([kp[:, :, :-1], kp[:, :, 1:]], axis=-2)
            vc = jnp.concatenate([vp[:, :, :-1], vp[:, :, 1:]], axis=-2)
            qa = jnp.arange(C)
            ka = jnp.arange(2 * C)
            diff = C + qa[:, None] - ka[None, :]
            base = (diff >= 0) & (diff <= WINDOW)
            kv_pos = (jnp.arange(nc)[:, None] - 1) * C + ka[None, :]
            mask = base[None, :, :] & (kv_pos >= 0)[:, None, :]
            scores = jnp.einsum('bhncd,bhnkd->bhnck', qc, kc) * SCALE
            scores = jnp.where(mask[None, None], scores, -jnp.inf)
            attn = jax.nn.softmax(scores, axis=-1)
            out = jnp.einsum('bhnck,bhnkd->bhncd', attn, vc)
            return out.reshape(B, H, S, D)
        B, S, E = x.shape
        H, D = (NUM_HEADS, HEAD_DIM)
        qkv = x @ w_qkv.T
        qkv = qkv.reshape(B, S, 3, H, D).transpose(2, 0, 3, 1, 4)
        q, k, v = (qkv[0], qkv[1], qkv[2])
        o = _sliding_window_attention(q, k, v)
        o = o.transpose(0, 2, 1, 3).reshape(B, S, E)
        return o @ w_out.T

    def _L0_ffn_ref(x, rg_w, ru_w, extra_scale, extra_bias, Wg, Wu, Wd, Sg, Su, Sd):
        import jax, jax.numpy as jnp
        import numpy as np
        from jax import lax
        H = 256
        I = 176
        E = 16
        K = 4
        ISH = 2 * I
        B, S = (4, 256)

        def _router(xf, rg_w, ru_w, extra_scale, extra_bias):
            g = xf @ rg_w.T
            u = xf @ ru_w.T
            scores = jnp.abs(u * jax.nn.silu(g))
            probs = jax.nn.softmax(scores.astype(jnp.float32), axis=-1)
            biased = probs + extra_bias[None, :]
            _, idx = lax.top_k(biased, K)
            orig = 1.0 + probs * extra_scale[None, :]
            w = jnp.take_along_axis(orig, idx, axis=1).astype(xf.dtype)
            return (w, idx)
        shape = x.shape
        xf = x.reshape(-1, H)
        w, idx = _router(xf, rg_w, ru_w, extra_scale, extra_bias)
        coeff = jnp.einsum('tk,tke->te', w, jax.nn.one_hot(idx, E, dtype=w.dtype))

        def step(y, ew):
            wg, wu, wd, c = ew
            h = jax.nn.silu(xf @ wg.T) * (xf @ wu.T)
            return (y + h @ wd.T * c[:, None], None)
        y0 = jnp.zeros_like(xf)
        y, _ = lax.scan(step, y0, (Wg, Wu, Wd, coeff.T))
        z = jax.nn.silu(xf @ Sg.T) * (xf @ Su.T) @ Sd.T
        return (y + z).reshape(shape)
    x = L0_attn_x
    mod = (_silu(L0_c) @ L0_wmod).reshape(L0_c.shape[0], 6, 1, -1)
    sa, ca, ga, sb, cb, gb = (mod[:, 0], mod[:, 1], mod[:, 2], mod[:, 3], mod[:, 4], mod[:, 5])
    ga = (2 * (ga >= 0) - 1) * jnp.maximum(jnp.abs(ga), 0.25)
    gb = (2 * (gb >= 0) - 1) * jnp.maximum(jnp.abs(gb), 0.25)
    h = _layernorm(x, axis=-1) * (1 + ca) + sa
    x = x + ga * _L0_attn_ref(h, L0_attn_w_qkv, L0_attn_w_out)
    h = _layernorm(x, axis=-1) * (1 + cb) + sb
    x = x + gb * _L0_ffn_ref(h, L0_ffn_rg_w, L0_ffn_ru_w, L0_ffn_extra_scale, L0_ffn_extra_bias, L0_ffn_Wg, L0_ffn_Wu, L0_ffn_Wd, L0_ffn_Sg, L0_ffn_Su, L0_ffn_Sd)
    return x

_drawn_inputs = setup_inputs


def setup_inputs(seed=0):
    import zlib

    import numpy as np

    out = dict(_drawn_inputs(seed))
    spreads = {'L0_ffn_extra_scale': (0.0, 0.8), 'L0_ffn_extra_bias': (0.0, 0.8)}
    factors = {'L0_ffn_rg_w': 8.0,
     'L0_ffn_ru_w': 8.0,
     'L0_ffn_Wg': 8.0,
     'L0_ffn_Wu': 8.0,
     'L0_ffn_Wd': 8.0,
     'L0_ffn_Sg': 8.0,
     'L0_ffn_Su': 8.0,
     'L0_ffn_Sd': 8.0}
    for name, (base, spread) in spreads.items():
        noise = np.random.default_rng([zlib.crc32(name.encode()), seed]).standard_normal(out[name].shape)
        drawn = base * np.exp(spread * noise) if base else spread * noise
        out[name] = jnp.asarray(drawn.astype(out[name].dtype))
    for name, factor in factors.items():
        out[name] = (out[name] * factor).astype(out[name].dtype)
    return out
```

```python
from contextlib import ExitStack

import concourse.bass as bass
from concourse import mybir

P = 128
S_LEN, D = 2048, 256
HEADS, DH = 16, 16
CH = 64
KD = D // P
TILES = S_LEN // P
GROUPS = TILES // 2
NE, TOPK, FI = 16, 4, 176
FH = FI // 2
SH_I = 2 * FI
EPS = 1e-5
SCALE = 1.0 / DH ** 0.5
BIG = 2.0 ** 100
ROWS = 3 * DH
VALID = 2 * ROWS
MASKS = 2 * (CH - 1)
WIN = 3 * CH
CAP = S_LEN + P
STEPS = (S_LEN * TOPK + NE * (P - 1)) // P
ONE_V = 2 * DH
VC = ONE_V + 1
STEPS_RUN = -(-STEPS // 4) * 4
RING = 4
TB_PAD, TB_COL = 9, 22
SH_OPS, FIN = 5, 1 + TOPK

F32 = mybir.dt.float32
F32R = mybir.dt.float32r
U32 = mybir.dt.uint32
I32 = mybir.dt.int32
ALU = mybir.AluOpType
ACT = mybir.ActivationFunctionType
AX = mybir.AxisListType


def plain(eng):
    eng.nop(nofuse=True)


def for_tiles(eng, body):
    for t in range(4):
        body(t, t, t // 2, 0)
    with eng.Fori(1, TILES // 4 - 1) as i:
        for t in range(4):
            body(4 * i + t, t, 2 * i + t // 2, i)
    last = TILES // 4 - 1
    for t in range(4):
        body(4 * last + t, t, 2 * last + t // 2, last)


def for_steps(eng, body, count):
    for t in range(4):
        body(t, t, 0)
    with eng.Fori(1, count // 4 - 1) as i:
        for t in range(4):
            body(4 * i + t, t, i)
    for t in range(4):
        body(count - 4 + t, t, count // 4 - 1)


def runs(n, low, high=None):
    return not isinstance(n, int) or (n >= low and (high is None or n <= high))


class Chain:

    def __init__(self, eng, sem, base):
        self.eng, self.sem, self.base, self.k = eng, sem, base, 0

    def mark(self, ins):
        ins.then_inc(self.sem, 1)
        self.k += 1
        return self

    def wait(self, is_plain=False):
        self.eng.wait_ge(self.sem, self.base + self.k)
        if is_plain:
            plain(self.eng)


def attention_and_routing(nc, A, T, ctx, own):

    def sb(name, shape, dt=F32):
        return ctx.enter_context(nc.sbuf_tensor(name, shape, dt))

    def pb(name, shape):
        return ctx.enter_context(nc.psum_tensor(name, shape, F32))

    def sem(name):
        return own.enter_context(nc.semaphore(name))

    def sems(name, n):
        return [sem(f"{name}{i}") for i in range(n)]

    ident, iota_e, pack = T["ident"], T["iota_e"], T["pack"]

    c_in = sb("c_in", [P, KD])
    c_tmp = sb("c_tmp", [P, 4, KD])
    c_col = sb("c_col", [P, KD, P])
    wmod = sb("wmod", [P, KD, 6 * D])
    ones_f = sb("ones_f", [P, P])
    mod = sb("mod", [P, 4, D])
    gates = sb("gates", [P, 2, D])
    g_tmp = sb("g_tmp", [P, 3, D])
    w_raw = sb("w_raw", [P, KD, 4 * D])
    w_hl = sb("w_hl", [P, KD, 2, 4 * D], F32R)
    r_raw = sb("r_raw", [P, KD, 2 * NE])
    r_hl = sb("r_hl", [P, KD, 2, 2 * NE], F32R)
    esc = sb("esc", [P, 2, NE])
    mk_raw = sb("mk_raw", [MASKS + 1, 2, P])
    mask_key = sb("mask_key", [MASKS + 1, P], F32R)
    mask_qry = sb("mask_qry", [MASKS, P], F32R)
    tri_raw = sb("tri_raw", [P, 2, P])
    tri = sb("tri", [P, 2, P], F32R)
    kval = sb("kval", [HEADS, 2, WIN], F32R)

    x_in = sb("x_in", [P, 2, 2, D])
    x_res = sb("x_res", [P, 4, D])
    x1 = sb("x1", [P, 4, D])
    ln_st = sb("ln_st", [P, 2, 2, 6])
    ln_mv = sb("ln_mv", [P, 2, 2, 2])
    ln_rs = sb("ln_rs", [P, 2, 2])
    ln_nm = sb("ln_nm", [P, 2, 2])
    ln_nw = sb("ln_nw", [P, 2, 4, 2])
    xn1 = sb("xn1", [P, 2, D])
    h1t = sb("h1t", [P, 2, D])
    h1 = sb("h1", [P, 2, D])
    hT = sb("hT", [P, 2, KD, 2, 2, WIN], F32R)
    q_ev = sb("q_ev", [P, 2, 2, 2 * P], F32R)
    k_ev = sb("k_ev", [P, 2, 2, 2 * WIN], F32R)
    Q2 = [sb(f"Q2_{i}", [VALID + 1, HEADS, 2, P], F32R) for i in range(2)]
    K2 = [sb(f"K2_{i}", [VALID + 1, HEADS, WIN], F32R) for i in range(2)]
    VW = sb("VW", [P, 4, HEADS, VC])
    neg_m = sb("neg_m", [P, 2, HEADS])
    mT = sb("mT", [HEADS, 2, P], F32R)
    MM = [sb(f"MM_{i}", [MASKS + 1, HEADS * P], F32R) for i in range(2)]
    prob = sb("prob", [P, 4, 4 * P])
    rden = sb("rden", [P, 2, 8])
    o_n = sb("o_n", [P, D])
    oT = sb("oT", [P, 2, KD, P], F32R)
    xn2 = sb("xn2", [P, D])
    h2t = sb("h2t", [P, D])
    h2 = sb("h2", [P, 4, D])
    h2T = sb("h2T", [P, 4, 2, KD, P], F32R)

    rt = sb("rt", [P, 10, 2, NE])
    r_sm = sb("r_sm", [P, 3, 2])
    top8 = sb("top8", [P, 2, 8])
    top8i = sb("top8i", [P, 2, 8], U32)
    pk = sb("pk", [P, 2, 2, 3 * TOPK])
    onehot = sb("onehot", [P, 2, 2, TOPK, NE])
    ohw = sb("ohw", [P, 2, TOPK, NE])
    ohs = sb("ohs", [P, 2, TOPK, NE])
    rank_f = sb("rank_f", [P, 2, NE])
    mask_e = sb("mask_e", [P, 2, 2, NE], F32R)
    msum = sb("msum", [P, 2, 2, NE], F32R)
    slot_u = sb("slot_u", [P, 2, 2, TOPK], U32)

    X, Y = pb("X", [P, 512]), pb("Y", [P, 512])
    SB = [pb(f"SB{i}", [P, 512]) for i in range(2)]
    TB = [pb(f"TB{i}", [P, 512]) for i in range(2)]
    O = pb("O", [P, 2, 512])

    c_ld, wm_ld, w_ld, k_ld, e_ld = sem("c_ld"), sems("wm_ld", 2), sem("w_ld"), sem("k_ld"), sem("e_ld")
    c_exp, c_dve, c_col_done = sem("c_exp"), sem("c_dve"), sem("c_col_done")
    mod_mm, mod_cp, gate_dve = sem("mod_mm"), sem("mod_cp"), sem("gate_dve")
    w_hi, w_lo, wo_dve, wo_hi, cst = sem("w_hi"), sem("w_lo"), sem("wo_dve"), sem("wo_hi"), sem("cst")
    pre_pool, kv_st = sem("pre_pool"), sem("kv_st")
    xin_ld, xres_ld = sems("xin_ld", 2), sems("xres_ld", 4)
    ln1_dve, ln1_act, ln1_mod, h1_ready = [sem(x) for x in ("ln1_dve", "ln1_act", "ln1_mod", "h1_ready")]
    th1_mm, hT_hi, hT_lo, carry = sem("th1_mm"), sem("hT_hi"), sem("hT_lo"), sem("carry")
    qk_mm, qk_hi, qk_lo, qk_st, qk_ld = [sem(x) for x in ("qk_mm", "qk_hi", "qk_lo", "qk_st", "qk_ld")]
    v_mm, v_ev = sem("v_mm"), sem("v_ev")
    s_mm, s_red, mt_mm, mt_cp = sem("s_mm"), sem("s_red"), sem("mt_mm"), sem("mt_cp")
    mm_ld = sems("mm_ld", 2)
    st_mm, exp_done, pv_mm, nrm = sem("st_mm"), sem("exp_done"), sem("pv_mm"), sem("nrm")
    to_mm, oT_hi, oT_lo, out_mm = sem("to_mm"), sem("oT_hi"), sem("oT_lo"), sem("out_mm")
    ln2_dve, ln2_act, ln2_mod, h2_ready = [sem(x) for x in ("ln2_dve", "ln2_act", "ln2_mod", "h2_ready")]
    th2_mm, h2T_hi, h2T_lo = sem("th2_mm"), sem("h2T_hi"), sem("h2T_lo")
    x1_st, h2_st, disp = sems("x1_st", 4), sems("h2_st", 4), sems("disp", 4)
    r_mm, r_act, r_dve, rank_mm, p_dve = [sem(x) for x in ("r_mm", "r_act", "r_dve", "rank_mm", "p_dve")]
    z_set = sem("z_set")
    cnt_mm, cnt_cp = sem("cnt_mm"), sem("cnt_cp")
    R_OPS, P_OPS, L1_OPS, L2_OPS = 24, 5, 16, 15
    LD = 19 * 16
    block = ctx.enter_context(nc.Block())

    x_t = A["x"].rearrange("(c n q) d -> n c q d", c=2, n=TILES)
    q_scr, k_scr = T["q_scr"], T["k_scr"]

    def three(eng, out, pairs):
        for i, (l_hi, l_lo, r_hi, r_lo) in enumerate(pairs):
            for j, (a, b) in enumerate(((l_hi, r_hi), (l_lo, r_hi), (l_hi, r_lo))):
                mm = eng.matmul(out, a, b, start=(i + j == 0), stop=(i == len(pairs) - 1 and j == 2))
        return mm

    @block.sync
    def _(eng):
        eng.dma_start(c_in[:, :], A["c"]).then_inc(c_ld, 16)

        def load_in(tiles, par):
            for j, n in enumerate(tiles):
                for c in range(2):
                    src = x_t[n, c] if not isinstance(n, int) or n >= 0 else (A["x"][0:CH, :], x_t[TILES - 1, 0])[c]
                    eng.dma_start(x_in[c * CH:(c + 1) * CH, par, j, :], src).then_inc(xin_ld[par], 16)

        load_in((-1, -1), 1)
        load_in((0, 1), 0)
        eng.dma_start(wmod[:, :, 0:2 * D], A["wmod"][:, :, 0:2 * D]).then_inc(wm_ld[0], 16)
        eng.dma_start(ident[:, :], A["ident"]).then_inc(k_ld, 16)
        eng.dma_start(tri_raw[:, :, :], A["tris"]).then_inc(k_ld, 16)
        eng.dma_start(mk_raw[:, :, :], A["masks"]).then_inc(k_ld, 16)
        eng.dma_start(iota_e[:, :, :], A["iotas"]).then_inc(k_ld, 16)
        eng.wait_ge(ln1_act, 2)
        load_in((2, 3), 1)
        eng.wait_ge(pre_pool, 6)
        for g in range(GROUPS):
            eng.dma_start(T["kv_scr"][g], kval[:, 0 if g == 0 else 1, :].bitcast(F32)).then_inc(kv_st, 16)
        eng.wait_ge(kv_st, 16 * GROUPS)

        def store_load_qk(g, n, par):
            eng.wait_ge(qk_lo, 4 * g + 4)
            plain(eng)
            eng.dma_start(q_scr[g].rearrange("l m p x -> p l m x"), q_ev[:, :, :, :].bitcast(F32)).then_inc(qk_st, 16)
            eng.dma_start(k_scr[g].rearrange("l m p x -> p l m x"), k_ev[:, :, :, :].bitcast(F32)).then_inc(qk_st, 16)
            eng.wait_ge(qk_st, 32 * g + 32)
            plain(eng)
            if runs(n, 4):
                eng.wait_ge(st_mm, 4 * n - 8)
                plain(eng)
            for c in range(2):
                for r in range(3):
                    p0 = c * ROWS + r * DH
                    q_rows = q_scr[g, r % 2].rearrange("m (h d) (c j x) -> c d (m h) j x", d=DH, c=2, j=2)
                    k_rows = k_scr[g, r // 2].rearrange("m (h d) (c x) -> c d (m h) x", d=DH, c=2)
                    for j in range(2):
                        eng.dma_start(Q2[par][p0:p0 + DH, :, j, c * CH:(c + 1) * CH].bitcast(F32),
                                      q_rows[c, :, :, j]).then_inc(qk_ld, 16)
                    eng.dma_start(K2[par][p0:p0 + DH, :, :].bitcast(F32), k_rows[c]).then_inc(qk_ld, 16)
            eng.dma_start(K2[par][VALID:VALID + 1, :, :].bitcast(F32), T["kv_scr"][g]).then_inc(qk_ld, 16)

        def put_max(n, e, p2):
            eng.wait_ge(mt_cp, n + 1)
            plain(eng)
            if runs(n, 2):
                eng.wait_ge(st_mm, 4 * n - 4)
            eng.dma_start(MM[p2][MASKS:MASKS + 1, :].bitcast(F32).rearrange("o (h x) -> o h x", h=HEADS),
                          mT[:, p2, :].bitcast(F32)).then_inc(mm_ld[p2], 16)

        def keep(n, t):
            eng.wait_ge(ln2_dve, L2_OPS * n + 1)
            plain(eng)
            eng.dma_start(T["x1_scr"][n], x1[:, t, :]).then_inc(x1_st[t], 16)
            eng.wait_ge(h2_ready, n + 1)
            plain(eng)
            eng.dma_start(T["h2_scr"][n], h2[:, t, :]).then_inc(h2_st[t], 16)

        eng.wait_ge(cst, 5)
        store_load_qk(0, 0, 0)
        put_max(0, 0, 0)

        def tile(n, t, e, i):
            if t % 2 == 0 and runs(n, 0, TILES - 5):
                eng.wait_ge(ln1_act, 2 * e + 4)
                plain(eng)
                load_in((n + 4, n + 5), (t // 2) % 2)
            if runs(n, 4):
                eng.wait_ge(ln2_dve, L2_OPS * (n - 4) + 1)
                plain(eng)
            for c in range(2):
                eng.dma_start(x_res[c * CH:(c + 1) * CH, t, :], x_t[n, c]).then_inc(xres_ld[t], 16)
            if t % 2 == 0 and runs(n, 0, TILES - 3):
                store_load_qk(e + 1, n + 2, (t // 2 + 1) % 2)
            if runs(n, 0, TILES - 2):
                put_max(n + 1, e + t % 2, (t + 1) % 2)
            if runs(n, 1):
                keep(n - 1, (t - 1) % 4)

        for_tiles(eng, tile)
        keep(TILES - 1, 3)
        for t in range(4):
            eng.wait_ge(x1_st[t], 16 * (TILES // 4) + 16)
            eng.wait_ge(h2_st[t], 16 * (TILES // 4) + 16)
            eng.wait_ge(disp[t], 16 * TOPK * (TILES // 4) + 16)

    @block.scalar
    def _(eng):
        for j, w in enumerate(("wq", "wk", "wv", "wo")):
            eng.dma_start(w_raw[:, :, j * D:(j + 1) * D], A[w]).then_inc(w_ld, 16)
        eng.dma_start(wmod[:, :, 2 * D:6 * D], A["wmod"][:, :, 2 * D:6 * D]).then_inc(wm_ld[1], 16)
        eng.dma_start(r_raw[:, :, 0:NE], A["rg"]).then_inc(e_ld, 16)
        eng.dma_start(r_raw[:, :, NE:2 * NE], A["ru"]).then_inc(e_ld, 16)
        eng.dma_start(esc[:, 0, :], A["escale"].partition_broadcast(P)).then_inc(e_ld, 16)
        eng.dma_start(esc[:, 1, :], A["ebias"].partition_broadcast(P)).then_inc(e_ld, 16)
        eng.wait_ge(c_ld, 16)
        eng.activation(c_tmp[:, 0, :], c_in[:, :], ACT.Exp, scale=-1.0).then_inc(c_exp, 1)

        def ln1_apply(g, par):
            eng.wait_ge(ln1_dve, L1_OPS * (g + 2))
            if not isinstance(g, int) or g >= 0:
                eng.wait_ge(ln1_mod, g + 1)
            for j in range(2):
                eng.activation(xn1[:, j, :], x_in[:, par, j, :], ACT.Identity, bias=ln_nm[:, 0, j:j + 1],
                               scale=ln_rs[:, 0, j:j + 1]).then_inc(ln1_act, 1)

        def hT_hi_part(g, par, bank, tiles):
            eng.wait_ge(th1_mm, g + 2)
            if not isinstance(g, int) or g >= 1:
                eng.wait_ge(carry, g)
            v = bank[:, :].rearrange("p (j k c q) -> p j k c q", j=2, k=KD, c=2)
            for j in tiles:
                eng.activation(hT[:, par, :, 0, :, CH * (1 + j):CH * (2 + j)], v[:, j], ACT.Copy).then_inc(hT_hi, 1)

        def qk_hi_part(g):
            if not isinstance(g, int) or g >= 1:
                eng.wait_ge(qk_st, 32 * g)
            for j, (ev, bank) in enumerate(((q_ev, X), (q_ev, Y), (k_ev, X), (k_ev, Y))):
                eng.wait_ge(qk_mm, 4 * g + j + 1)
                w = ev.shape[3]
                eng.activation(ev[:, 0, j % 2, :], bank[:, 0:w], ACT.Copy).then_inc(qk_hi, 1)

        def v_out(n, t, bank):
            eng.wait_ge(v_mm, n + 1)
            if runs(n, 4):
                eng.wait_ge(pv_mm, 4 * n - 12)
            eng.activation(VW[:, t, :, 0:2 * DH].rearrange("p h (w d) -> p w h d", w=2),
                           bank[:, :].rearrange("p (w h d) -> p w h d", w=2, h=HEADS), ACT.Copy).then_inc(v_ev, 1)

        def max_out(n, e, p2, bank):
            eng.wait_ge(mt_mm, n + 1)
            if runs(n, 2):
                eng.wait_ge(mm_ld[p2], 16 * e)
            eng.activation(mT[:, p2, :], bank[0:HEADS, 0:P], ACT.Copy).then_inc(mt_cp, 1)

        ln1_apply(-1, 1)
        ln1_apply(0, 0)
        eng.wait_ge(w_ld, 64)
        eng.activation(w_hl[:, :, 0, 0:3 * D], w_raw[:, :, 0:3 * D], ACT.Copy).then_inc(w_hi, 1)
        hT_hi_part(-1, 1, X, (1,))
        hT_hi_part(0, 0, Y, (0, 1))
        qk_hi_part(0)
        v_out(0, 0, X)
        v_out(1, 1, Y)
        ln1_apply(1, 1)
        eng.wait_ge(wo_dve, KD)
        eng.activation(w_hl[:, :, 0, 3 * D:4 * D], w_raw[:, :, 3 * D:4 * D], ACT.Copy).then_inc(wo_hi, 1)
        max_out(0, 0, 0, X)

        def tile(n, t, e, i):
            m, tm = n - 1, (t - 1) % 4
            if runs(n, 1):
                eng.wait_ge(to_mm, m + 1)
                eng.activation(oT[:, 0, :, :], X[:, 0:D].rearrange("p (k x) -> p k x", k=KD), ACT.Copy).then_inc(oT_hi, 1)
            if t % 2 == 0 and runs(n, 0, TILES - 3):
                hT_hi_part(e + 1, (t // 2 + 1) % 2, Y, (0, 1))
                qk_hi_part(e + 1)
            if t % 2 == 1 and runs(n, 0, TILES - 2):
                v_out(n + 1, (t + 1) % 4, Y)
                v_out(n + 2, (t + 2) % 4, X)
            if t % 2 == 1 and runs(n, 3):
                router_exp(e - 1, 0, X)
            for q in range(4):
                eng.wait_ge(st_mm, 4 * n + q + 1)
                if runs(n, 1):
                    eng.wait_ge(pv_mm, 4 * n + q - 3)
                eng.activation(prob[:, q, :], TB[q % 2][:, :], ACT.Exp, scale=SCALE).then_inc(exp_done, 1)
                if q == 2 and t % 2 == 1 and runs(n, 3):
                    router_exp(e - 1, 1, X)
                if q == 1 and runs(n, 1):
                    eng.wait_ge(ln2_dve, L2_OPS * (m + 1))
                    eng.wait_ge(ln2_mod, m)
                    eng.activation(xn2[:, :], x1[:, tm, :], ACT.Identity, bias=ln_nm[:, 1, 0:1],
                                   scale=ln_rs[:, 1, 0:1]).then_inc(ln2_act, 1)
            if runs(n, 0, TILES - 2):
                max_out(n + 1, e + t % 2, (t + 1) % 2, (X, Y)[t % 2])
            if runs(n, 1):
                h2T_hi_part(m, tm, (Y, X)[t % 2])
            if t % 2 == 1 and runs(n, 0, TILES - 5):
                ln1_apply(e + 2, (t // 2) % 2)

        def h2T_hi_part(m, tm, bank):
            eng.wait_ge(th2_mm, m + 1)
            eng.activation(h2T[:, tm, 0, :, :], bank[:, 0:D].rearrange("p (k x) -> p k x", k=KD), ACT.Copy).then_inc(h2T_hi, 1)

        def router_exp(g, part, bank):
            if part == 0:
                eng.wait_ge(r_mm, g + 1)
                v = bank[:, 0:4 * NE].rearrange("p (a u x) -> p a u x", a=2, u=2)
                if not isinstance(g, int) or g >= 1:
                    eng.wait_ge(r_dve, R_OPS * g)
                eng.activation(rt[:, 0, :, :], v[:, :, 0, :], ACT.Exp, scale=-1.0).then_inc(r_act, 1)
            else:
                eng.wait_ge(r_dve, R_OPS * g + 7)
                eng.activation(rt[:, 6, :, :], rt[:, 5, :, :], ACT.Exp).then_inc(r_act, 1)

        for_tiles(eng, tile)
        m = TILES - 1
        eng.wait_ge(to_mm, m + 1)
        eng.activation(oT[:, 0, :, :], Y[:, 0:D].rearrange("p (k x) -> p k x", k=KD), ACT.Copy).then_inc(oT_hi, 1)
        eng.wait_ge(ln2_dve, L2_OPS * (m + 1))
        eng.wait_ge(ln2_mod, m)
        eng.activation(xn2[:, :], x1[:, 3, :], ACT.Identity, bias=ln_nm[:, 1, 0:1],
                       scale=ln_rs[:, 1, 0:1]).then_inc(ln2_act, 1)
        h2T_hi_part(m, 3, X)
        router_exp(GROUPS - 1, 0, Y)
        router_exp(GROUPS - 1, 1, Y)

    @block.gpsimd
    def _(eng):
        for t in range(4):
            for credit in (x1_st[t], h2_st[t]):
                eng.nop(nofuse=True).then_inc(credit, 16)
        eng.memset(T["zeros"][:, :], 0.0).then_inc(z_set, 1)
        eng.wait_ge(z_set, 1)
        for t in range(4):
            r = P // 4 * t
            eng.dma_start(T["xs_scr"][NE * CAP + r:NE * CAP + r + P // 4, :],
                          T["zeros"][r:r + P // 4, :]).then_inc(disp[t], 16)
        for i in range(2):
            eng.memset(Q2[i][:, :, :, :].bitcast(F32), 0.0).then_inc(pre_pool, 1)
        eng.memset(kval[:, :, :].bitcast(F32), 0.0).then_inc(pre_pool, 1)
        eng.wait_ge(pre_pool, 3)
        for i in range(2):
            eng.memset(Q2[i][VALID:VALID + 1, :, :, 0:CH].bitcast(F32), 1.0).then_inc(pre_pool, 1)
        eng.memset(kval[:, 0, 0:CH].bitcast(F32), -BIG).then_inc(pre_pool, 1)
        eng.wait_ge(pre_pool, 6)

        def ln1_modulate(g):
            eng.wait_ge(ln1_act, 2 * g + 4)
            if not isinstance(g, int) or g >= 0:
                eng.wait_ge(h1_ready, g + 1)
            eng.tensor_tensor(h1t[:, :, :], xn1[:, :, :], mod[:, 1:2, :].broadcast_to([P, 2, D]), ALU.mult).then_inc(ln1_mod, 1)
            eng.wait_ge(ln1_mod, g + 2)
            if not isinstance(g, int) or g >= 0:
                eng.wait_ge(th1_mm, g + 1)
            eng.tensor_tensor(h1[:, :, :], h1t[:, :, :], mod[:, 0:1, :].broadcast_to([P, 2, D]), ALU.add).then_inc(h1_ready, 1)

        def carry_on(g, par):
            eng.wait_ge(hT_lo, 2 * g + 1)
            if not isinstance(g, int) or g >= 2:
                eng.wait_ge(v_mm, 2 * g - 2)
            plain(eng)
            a = hT[:, par].rearrange("p k l c x -> p (k l c) x")
            b = hT[:, 1 - par].rearrange("p k l c x -> p (k l c) x")
            eng.tensor_copy(a[:, :, 0:CH], b[:, :, 2 * CH:3 * CH]).then_inc(carry, 1)

        def ln2_modulate(m, tm, im):
            eng.wait_ge(ln2_act, m + 1)
            if runs(m, 1):
                eng.wait_ge(h2_ready, m)
            eng.tensor_tensor(h2t[:, :], xn2[:, :], mod[:, 3, :], ALU.mult).then_inc(ln2_mod, 1)
            eng.wait_ge(ln2_mod, m + 1)
            if runs(m, 4):
                eng.wait_ge(th2_mm, m)
                eng.wait_ge(h2_st[tm], 16 * im + 16)
                eng.wait_ge(disp[tm], 16 * TOPK * im + 16)
            eng.tensor_tensor(h2[:, tm, :], h2t[:, :], mod[:, 2, :], ALU.add).then_inc(h2_ready, 1)

        def dispatch(g, t0, par):
            eng.wait_ge(p_dve, P_OPS * g + 4)
            plain(eng)
            for a in range(2):
                for k in range(TOPK):
                    eng.indirect_dma_start(T["xs_scr"], bass.IndirectOffsetOnAxis(ap=slot_u[:, par, a, k:k + 1], axis=0),
                                           h2[:, t0 + a, :], None).then_inc(disp[t0 + a], 16)

        eng.wait_ge(mod_cp, 2)
        ln1_modulate(-1)
        ln1_modulate(0)
        carry_on(0, 0)
        ln1_modulate(1)
        eng.wait_ge(mod_cp, 4)

        def tile(n, t, e, i):
            if t % 2 == 0 and runs(n, 0, TILES - 3):
                carry_on(e + 1, (t // 2 + 1) % 2)
            if runs(n, 1):
                ln2_modulate(n - 1, (t - 1) % 4, i if t else i - 1)
            if t % 2 == 0 and runs(n, 4):
                dispatch(e - 2, t, (t // 2) % 2)
            if t % 2 == 1 and runs(n, 0, TILES - 5):
                ln1_modulate(e + 2)

        for_tiles(eng, tile)
        ln2_modulate(TILES - 1, 3, TILES // 4 - 1)
        dispatch(GROUPS - 2, 0, 0)
        dispatch(GROUPS - 1, 2, 1)

    @block.vector
    def _(eng):
        def f(ap):
            return ap.bitcast(F32)

        eng.memset(ones_f[:, :], 1.0).then_inc(c_dve, 1)
        ch = Chain(eng, c_dve, 1)
        eng.wait_ge(c_exp, 1)
        ch.mark(eng.tensor_scalar(c_tmp[:, 1, :], c_tmp[:, 0, :], 1.0, None, ALU.add)).wait()
        ch.mark(eng.reciprocal(c_tmp[:, 2, :], c_tmp[:, 1, :])).wait()
        ch.mark(eng.tensor_tensor(c_tmp[:, 3, :], c_in[:, :], c_tmp[:, 2, :], ALU.mult)).wait()
        for k in range(KD):
            eng.tensor_scalar(c_col[:, k, :], ones_f[:, :], c_tmp[:, 3, k:k + 1], None, ALU.mult).then_inc(c_col_done, 1)

        def rstd(ch, which, w):
            v, y, a, b = [ln_nw[:, which, i, 0:w] for i in range(4)]
            ch.mark(eng.tensor_scalar(v, ln_mv[:, which, 0:w, 1], EPS, None, ALU.add)).wait()
            ch.mark(eng.tensor_scalar(y.bitcast(I32), v.bitcast(I32), -0.5, float(0x5F3759DF), ALU.mult, ALU.add)).wait()
            for i in range(3):
                ch.mark(eng.scalar_tensor_tensor(out=a, in0=y, scalar=-0.5, in1=y, op0=ALU.mult, op1=ALU.mult)).wait()
                ch.mark(eng.tensor_tensor(b, a, v, ALU.mult)).wait()
                to = ln_rs[:, which, 0:w] if i == 2 else y
                ch.mark(eng.scalar_tensor_tensor(out=to, in0=b, scalar=1.5, in1=y, op0=ALU.add, op1=ALU.mult)).wait()
            ch.mark(eng.scalar_tensor_tensor(out=ln_nm[:, which, 0:w], in0=ln_mv[:, which, 0:w, 0], scalar=-1.0,
                                             in1=ln_rs[:, which, 0:w], op0=ALU.mult, op1=ALU.mult))

        def ln1_stats(g, par, count):
            ch = Chain(eng, ln1_dve, L1_OPS * (g + 1))
            eng.wait_ge(xin_ld[par], 64 * count)
            if not isinstance(g, int) or g >= 0:
                eng.wait_ge(ln1_act, 2 * g + 2)
                ch.wait()
            plain(eng)
            for j in range(2):
                ch.mark(eng.bn_stats(ln_st[:, 0, j, :], x_in[:, par, j, :]))
            ch.wait(True)
            for j in range(2):
                ch.mark(eng.bn_aggr(ln_mv[:, 0, j, :], ln_st[:, 0, j, :]))
            ch.wait()
            rstd(ch, 0, 2)
            assert ch.k == L1_OPS

        def hT_lo_part(g, par, bank, tiles):
            v = bank[:, :].rearrange("p (j k c q) -> p j k c q", j=2, k=KD, c=2)
            eng.wait_ge(hT_hi, 2 * g + 3)
            for j in tiles:
                eng.tensor_tensor(hT[:, par, :, 1, :, CH * (1 + j):CH * (2 + j)], v[:, j],
                                  f(hT[:, par, :, 0, :, CH * (1 + j):CH * (2 + j)]), ALU.subtract).then_inc(hT_lo, 1)

        def qk_lo_part(g):
            for j, (ev, bank) in enumerate(((q_ev, X), (q_ev, Y), (k_ev, X), (k_ev, Y))):
                eng.wait_ge(qk_hi, 4 * g + j + 1)
                w = ev.shape[3]
                eng.tensor_tensor(ev[:, 1, j % 2, :], bank[:, 0:w], f(ev[:, 0, j % 2, :]), ALU.subtract).then_inc(qk_lo, 1)

        def row_max(n, p2, q):
            eng.wait_ge(s_mm, 4 * n + q + 1)
            if q == 0 and runs(n, 2):
                eng.wait_ge(mt_mm, n - 1)
            eng.tensor_reduce(neg_m[:, p2, 4 * q:4 * q + 4], SB[q % 2][:, :].rearrange("p (h x) -> p h x", h=4),
                              AX.X, ALU.max, negate=True).then_inc(s_red, 1)

        ln1_stats(-1, 1, 1)
        ln1_stats(0, 0, 1)
        eng.wait_ge(mod_mm, 1)
        eng.tensor_scalar(mod[:, 0, :], SB[0][:, 0:D], 1.0, None, ALU.mult).then_inc(mod_cp, 1)
        eng.tensor_scalar(mod[:, 1, :], SB[0][:, D:2 * D], 1.0, None, ALU.add).then_inc(mod_cp, 1)
        eng.wait_ge(w_hi, 1)
        eng.tensor_tensor(w_hl[:, :, 1, 0:3 * D], w_raw[:, :, 0:3 * D], f(w_hl[:, :, 0, 0:3 * D]), ALU.subtract).then_inc(w_lo, 1)
        eng.wait_ge(k_ld, 64)
        eng.tensor_copy(mask_key[:, :], mk_raw[:, 0, :]).then_inc(cst, 1)
        eng.tensor_copy(mask_qry[:, :], mk_raw[0:MASKS, 1, :]).then_inc(cst, 1)
        eng.tensor_copy(tri[:, :, :], tri_raw[:, :, :]).then_inc(cst, 1)
        for i in range(2):
            eng.tensor_copy(MM[i][0:MASKS, :].rearrange("p (h x) -> p h x", h=HEADS),
                            mk_raw[0:MASKS, 1:2, :].broadcast_to([MASKS, HEADS, P])).then_inc(cst, 1)
        eng.memset(VW[:, :, :, ONE_V:VC], 1.0).then_inc(cst, 1)
        eng.memset(msum[:, 0, 0, :].bitcast(F32), 0.0).then_inc(cst, 1)
        eng.wait_ge(e_ld, 64)
        eng.tensor_copy(r_hl[:, :, 0, :], r_raw[:, :, :]).then_inc(cst, 1)
        eng.wait_ge(cst, 8)
        eng.tensor_tensor(r_hl[:, :, 1, :], r_raw[:, :, :], f(r_hl[:, :, 0, :]), ALU.subtract).then_inc(cst, 1)
        hT_lo_part(-1, 1, X, (1,))
        hT_lo_part(0, 0, Y, (0, 1))
        qk_lo_part(0)
        ln1_stats(1, 1, 2)
        eng.wait_ge(mod_mm, 3)
        eng.tensor_scalar(mod[:, 2, :], SB[1][:, D:2 * D], 1.0, None, ALU.mult).then_inc(mod_cp, 1)
        eng.tensor_scalar(mod[:, 3, :], TB[0][:, 0:D], 1.0, None, ALU.add).then_inc(mod_cp, 1)
        for i, raw in enumerate((SB[1][:, 0:D], TB[0][:, D:2 * D])):
            ch = Chain(eng, gate_dve, 5 * i)
            if i:
                ch.wait()
            ch.mark(eng.tensor_scalar(g_tmp[:, 2, :], raw, -1.0, 0.25, ALU.mult, ALU.max))
            ch.mark(eng.tensor_scalar(g_tmp[:, 1, :], raw, 0.0, 2.0, ALU.is_ge, ALU.mult)).wait()
            ch.mark(eng.tensor_tensor(g_tmp[:, 0, :], raw, g_tmp[:, 2, :], ALU.max)).wait()
            eng.scalar_tensor_tensor(out=(gates[:, 0, :], T["gb"][:, :])[i], in0=g_tmp[:, 1, :], scalar=-1.0,
                                     in1=g_tmp[:, 0, :], op0=ALU.add, op1=ALU.mult).then_inc(gate_dve, 2)
        eng.wait_ge(gate_dve, 5)
        for k in range(KD):
            eng.tensor_tensor(w_raw[:, k, 3 * D:4 * D], w_raw[:, k, 3 * D:4 * D], gates[:, 0, :], ALU.mult).then_inc(wo_dve, 1)
        eng.wait_ge(wo_hi, 1)
        eng.tensor_tensor(w_hl[:, :, 1, 3 * D:4 * D], w_raw[:, :, 3 * D:4 * D], f(w_hl[:, :, 0, 3 * D:4 * D]),
                          ALU.subtract).then_inc(w_lo, 1)
        for q in range(4):
            row_max(0, 0, q)

        def normalise(m):
            eng.wait_ge(pv_mm, 4 * m + 4)
            if runs(m, 1):
                eng.wait_ge(to_mm, m)
            v = O[:, :, 0:8 * VC].rearrange("p b (h x) -> p b h x", x=VC)
            eng.reciprocal(rden[:, :, :], v[:, :, :, ONE_V]).then_inc(nrm, 1)
            eng.wait_ge(nrm, 3 * m + 1)
            for c in range(2):
                r = slice(c * CH, (c + 1) * CH)
                eng.tensor_tensor(o_n[r, :].rearrange("p (b h d) -> p b h d", b=2, h=8), v[r, :, :, c * DH:(c + 1) * DH],
                                  rden[r, :, :].unsqueeze(3).broadcast_to([CH, 2, 8, DH]), ALU.mult).then_inc(nrm, 1)

        def oT_lo_part(m, bank):
            eng.wait_ge(oT_hi, m + 1)
            eng.tensor_tensor(oT[:, 1, :, :], bank[:, 0:D].rearrange("p (k x) -> p k x", k=KD), f(oT[:, 0, :, :]),
                              ALU.subtract).then_inc(oT_lo, 1)

        def residual(m, tm, im, bank):
            eng.wait_ge(out_mm, m + 1)
            eng.wait_ge(xres_ld[tm], 32 * im + 32)
            if runs(m, 4):
                eng.wait_ge(x1_st[tm], 16 * im + 16)
                eng.wait_ge(ln2_act, m)
            ch = Chain(eng, ln2_dve, L2_OPS * m)
            ch.mark(eng.tensor_tensor(x1[:, tm, :], bank[:, 0:D], x_res[:, tm, :], ALU.add))
            if runs(m, 1):
                eng.wait_ge(ln2_act, m)
            ch.wait(True)
            ch.mark(eng.bn_stats(ln_st[:, 1, 0, :], x1[:, tm, :])).wait(True)
            ch.mark(eng.bn_aggr(ln_mv[:, 1, 0, :], ln_st[:, 1, 0, :])).wait()
            rstd(ch, 1, 1)
            assert ch.k == L2_OPS

        def h2T_lo_part(m, tm, bank):
            eng.wait_ge(h2T_hi, m + 1)
            eng.tensor_tensor(h2T[:, tm, 1, :, :], bank[:, 0:D].rearrange("p (k x) -> p k x", k=KD),
                              f(h2T[:, tm, 0, :, :]), ALU.subtract).then_inc(h2T_lo, 1)

        def b3(ap):
            return ap.unsqueeze(2).broadcast_to([P, 2, NE])

        def route_scores(g, bank):
            c = Chain(eng, r_dve, R_OPS * g)
            v = bank[:, 0:4 * NE].rearrange("p (a u x) -> p a u x", a=2, u=2)
            eng.wait_ge(r_act, 2 * g + 1)
            c.mark(eng.tensor_scalar(rt[:, 1, :, :], rt[:, 0, :, :], 1.0, None, ALU.add)).wait()
            c.mark(eng.reciprocal(rt[:, 2, :, :], rt[:, 1, :, :])).wait()
            c.mark(eng.tensor_tensor(rt[:, 3, :, :], v[:, :, 0, :], rt[:, 2, :, :], ALU.mult)).wait()
            c.mark(eng.tensor_tensor(rt[:, 4, :, :], v[:, :, 1, :], rt[:, 3, :, :], ALU.mult)).wait()
            c.mark(eng.scalar_tensor_tensor(out=rt[:, 9, :, :], in0=rt[:, 4, :, :], scalar=-1.0, in1=rt[:, 4, :, :],
                                            op0=ALU.mult, op1=ALU.max)).wait()
            c.mark(eng.tensor_reduce(r_sm[:, 0, :], rt[:, 9, :, :], AX.X, ALU.max, negate=True)).wait()
            c.mark(eng.tensor_tensor(rt[:, 5, :, :], rt[:, 9, :, :], b3(r_sm[:, 0, :]), ALU.add))
            assert c.k == 7

        def route(g, par):
            c = Chain(eng, r_dve, R_OPS * g + 7)
            eng.wait_ge(r_act, 2 * g + 2)
            c.mark(eng.tensor_reduce(r_sm[:, 1, :], rt[:, 6, :, :], AX.X, ALU.add)).wait()
            c.mark(eng.reciprocal(r_sm[:, 2, :], r_sm[:, 1, :])).wait()
            c.mark(eng.tensor_tensor(rt[:, 7, :, :], rt[:, 6, :, :], b3(r_sm[:, 2, :]), ALU.mult)).wait()
            c.mark(eng.tensor_tensor(rt[:, 8, :, :], rt[:, 7, :, :], esc[:, 1:2, :].broadcast_to([P, 2, NE]), ALU.add))
            c.wait(True)
            for a in range(2):
                c.mark(eng.max(top8[:, a, :], rt[:, 8, a, :]))
            c.wait(True)
            for a in range(2):
                c.mark(eng.max_index(top8i[:, a, :], top8[:, a, :], rt[:, 8, a, :]))
            c.wait()
            c.mark(eng.tensor_scalar(pk[:, par, :, 0:TOPK], top8i[:, :, 0:TOPK], 1.0, None, ALU.mult)).wait()
            c.mark(eng.tensor_tensor(onehot[:, par], pk[:, par, :, 0:TOPK].unsqueeze(3).broadcast_to([P, 2, TOPK, NE]),
                                     iota_e[:, 0:1, :].unsqueeze(1).broadcast_to([P, 2, TOPK, NE]), ALU.is_equal))
            c.mark(eng.tensor_tensor(rt[:, 3, :, :], rt[:, 7, :, :], esc[:, 0:1, :].broadcast_to([P, 2, NE]), ALU.mult)).wait()
            c.mark(eng.tensor_scalar(rt[:, 4, :, :], rt[:, 3, :, :], 1.0, None, ALU.add)).wait()
            c.mark(eng.tensor_tensor(ohw[:, :, :, :], onehot[:, par], rt[:, 4, :, :].unsqueeze(2).broadcast_to([P, 2, TOPK, NE]),
                                     ALU.mult)).wait()
            c.mark(eng.tensor_reduce(pk[:, par, :, 2 * TOPK:3 * TOPK], ohw[:, :, :, :], AX.X, ALU.add))
            if not isinstance(g, int) or g >= 1:
                eng.wait_ge(rank_mm, g)
            with nc.allow_low_precision(reason="zeros and ones"):
                c.mark(eng.tensor_reduce(mask_e[:, par], onehot[:, par].rearrange("p a k x -> p a x k"), AX.X, ALU.add)).wait()
            c.mark(eng.tensor_tensor(msum[:, par, 1, :], f(msum[:, par, 0, :]), f(mask_e[:, par, 0, :]), ALU.add)).wait()
            c.mark(eng.tensor_tensor(msum[:, 1 - par, 0, :], f(msum[:, par, 1, :]), f(mask_e[:, par, 1, :]), ALU.add))
            assert c.k == R_OPS - 7

        def place(g, n, par, bank, prev=None):
            c = Chain(eng, p_dve, P_OPS * g)
            eng.wait_ge(rank_mm, g + 1)
            v = bank[:, 0:2 * NE].rearrange("p (a x) -> p a x", a=2)
            c.mark(eng.tensor_tensor(rank_f[:, :, :], v, iota_e[:, 1:2, :].broadcast_to([P, 2, NE]), ALU.add)).wait()
            c.mark(eng.tensor_tensor(ohs[:, :, :, :], onehot[:, par], rank_f[:, :, :].unsqueeze(2).broadcast_to([P, 2, TOPK, NE]),
                                     ALU.mult)).wait()
            c.mark(eng.tensor_reduce(pk[:, par, :, TOPK:2 * TOPK], ohs[:, :, :, :], AX.X, ALU.add)).wait()
            if prev is not None:
                for t, count in prev:
                    eng.wait_ge(disp[t], count + 16)
            c.mark(eng.tensor_copy(slot_u[:, par, :, :], pk[:, par, :, TOPK:2 * TOPK]))
            c.mark(eng.tensor_scalar(pack[:, bass.ds(n, 2), :], pk[:, par], 1.0, None, ALU.mult)).wait()
            assert c.k == P_OPS

        def tile(n, t, e, i):
            m, tm, im = n - 1, (t - 1) % 4, i if t else i - 1
            if runs(n, 1):
                normalise(m)
                oT_lo_part(m, X)
            if t % 2 == 0 and runs(n, 0, TILES - 3):
                hT_lo_part(e + 1, (t // 2 + 1) % 2, Y, (0, 1))
                qk_lo_part(e + 1)
            if runs(n, 1):
                residual(m, tm, im, (X, Y)[t % 2])
            if t % 2 == 1 and runs(n, 3):
                route_scores(e - 1, X)
            if t % 2 == 0 and runs(n, 4):
                place(e - 2, n - 4, (t // 2) % 2, Y, [(t, 64 * (i - 1)), (t + 1, 64 * (i - 1))] if runs(n, 8) else None)
            for q in range(4):
                if runs(n, 0, TILES - 2):
                    row_max(n + 1, (t + 1) % 2, q)
            if t % 2 == 1 and runs(n, 3):
                route(e - 1, (t // 2 + 1) % 2)
            if runs(n, 1):
                h2T_lo_part(m, tm, (Y, X)[t % 2])
            if t % 2 == 1 and runs(n, 0, TILES - 5):
                ln1_stats(e + 2, (t // 2) % 2, i + 2 + t // 2)

        for_tiles(eng, tile)
        m, im = TILES - 1, TILES // 4 - 1
        normalise(m)
        oT_lo_part(m, Y)
        residual(m, 3, im, X)
        place(GROUPS - 2, TILES - 4, 0, Y, [(0, 64 * im), (1, 64 * im)])
        h2T_lo_part(m, 3, X)
        route_scores(GROUPS - 1, Y)
        route(GROUPS - 1, 1)
        place(GROUPS - 1, TILES - 2, 1, X, [(2, 64 * im), (3, 64 * im)])
        eng.wait_ge(cnt_mm, 1)
        eng.tensor_copy(T["count"][:, :], Y[:, 0:NE]).then_inc(cnt_cp, 1)

    @block.tensor
    def _(eng):
        banks = ((Y, X), (X, Y))

        def modulation(b, bank):
            for k in range(KD):
                mm = eng.matmul(bank[:, :], c_col[:, k, :], wmod[:, k, 2 * D * b:2 * D * (b + 1)], start=(k == 0),
                                stop=(k == KD - 1))
            mm.then_inc(mod_mm, 1)

        def transpose_h1(g, bank, tiles):
            eng.wait_ge(h1_ready, g + 2)
            for j in tiles:
                for k in range(KD):
                    o = (2 * j + k) * P
                    mm = eng.transpose(bank[:, o:o + P], h1[:, j, k * P:(k + 1) * P], ident[:, :])
            mm.then_inc(th1_mm, 1)

        def project_qk(g, par, own_bank=True):
            eng.wait_ge(hT_lo, 2 * g + 3)
            eng.wait_ge(carry, g + 1)
            for j, bank in enumerate((X, Y, X, Y)):
                if j >= 2:
                    eng.wait_ge(qk_lo, 4 * g + j - 1)
                col = (j // 2) * D + (j % 2) * P
                lo = CH if j < 2 else 0
                w = WIN - lo
                pairs = [(w_hl[:, k, 0, col:col + P], w_hl[:, k, 1, col:col + P],
                          hT[:, par, k, 0, :, lo:WIN], hT[:, par, k, 1, :, lo:WIN]) for k in range(KD)]
                three(eng, bank[:, 0:2 * w], pairs).then_inc(qk_mm, 1)

        def project_v(n, j, par, bank):
            for c in range(2):
                win = slice(CH * j, CH * (j + 2))
                mm = three(eng, bank[:, c * D:(c + 1) * D],
                           [(hT[:, par, k, 0, c, win], hT[:, par, k, 1, c, win],
                             w_hl[:, k, 0, 2 * D:3 * D], w_hl[:, k, 1, 2 * D:3 * D]) for k in range(KD)])
            mm.then_inc(v_mm, 1)

        def scores(n, j, par, q):
            if runs(n, 1) or q >= 2:
                eng.wait_ge(s_red, 4 * n + q - 1)
            bank = SB[q % 2]
            eng.matmul(bank[:, :].rearrange("p (h x) -> p h x", h=4), mask_qry[:, :],
                       mask_key[0:MASKS, :].unsqueeze(1).broadcast_to([MASKS, 4, P]), start=True, stop=True)
            for hh in range(4):
                mm = eng.matmul(bank[:, hh * P:(hh + 1) * P], Q2[par][:, 4 * q + hh, j, :],
                                K2[par][:, 4 * q + hh, CH * j:CH * (j + 2)], start=False, stop=True,
                                skip_group_check=True)
            mm.then_inc(s_mm, 1)

        def scores_t(n, j, par, p2, q):
            if runs(n, 1) or q >= 2:
                eng.wait_ge(exp_done, 4 * n + q - 1)
            bank = TB[q % 2]
            eng.matmul(bank[:, :], mask_key[:, :], MM[p2][:, 4 * P * q:4 * P * (q + 1)], start=True, stop=True)
            for hh in range(4):
                mm = eng.matmul(bank[:, hh * P:(hh + 1) * P], K2[par][:, 4 * q + hh, CH * j:CH * (j + 2)],
                                Q2[par][:, 4 * q + hh, j, :], start=False, stop=True,
                                skip_group_check=True)
            mm.then_inc(st_mm, 1)

        def weigh(n, t, q):
            eng.wait_ge(exp_done, 4 * n + q + 1)
            for hh in range(4):
                h = 4 * q + hh
                mm = eng.matmul(O[:, h // 8, (h % 8) * VC:(h % 8 + 1) * VC], prob[:, q, hh * P:(hh + 1) * P],
                                VW[:, t, h, :], start=True, stop=True)
            mm.then_inc(pv_mm, 1)

        def transpose_max(n, p2, bank):
            eng.wait_ge(s_red, 4 * n + 4)
            eng.transpose(bank[0:HEADS, 0:P], neg_m[:, p2, :], ident[:, :]).then_inc(mt_mm, 1)

        def transpose_o(m, bank):
            eng.wait_ge(nrm, 3 * m + 3)
            for k in range(KD):
                mm = eng.transpose(bank[:, k * P:(k + 1) * P], o_n[:, k * P:(k + 1) * P], ident[:, :])
            mm.then_inc(to_mm, 1)

        def project_out(m, bank):
            eng.wait_ge(oT_lo, m + 1)
            three(eng, bank[:, 0:D], [(oT[:, 0, k, :], oT[:, 1, k, :], w_hl[:, k, 0, 3 * D:4 * D],
                                       w_hl[:, k, 1, 3 * D:4 * D]) for k in range(KD)]).then_inc(out_mm, 1)

        def transpose_h2(m, tm, bank):
            eng.wait_ge(h2_ready, m + 1)
            for k in range(KD):
                mm = eng.transpose(bank[:, k * P:(k + 1) * P], h2[:, tm, k * P:(k + 1) * P], ident[:, :])
            mm.then_inc(th2_mm, 1)

        def router(g, t0, bank):
            eng.wait_ge(h2T_lo, 2 * g + 2)
            for a in range(2):
                mm = three(eng, bank[:, a * 2 * NE:(a + 1) * 2 * NE],
                           [(h2T[:, t0 + a, 0, k, :], h2T[:, t0 + a, 1, k, :], r_hl[:, k, 0, :], r_hl[:, k, 1, :])
                            for k in range(KD)])
            mm.then_inc(r_mm, 1)

        def ranks(g, par, bank):
            eng.wait_ge(r_dve, R_OPS * g + R_OPS)
            for a in range(2):
                eng.matmul(bank[:, a * NE:(a + 1) * NE], tri[:, 0, :], mask_e[:, par, a, :], start=True, stop=False)
                mm = eng.matmul(bank[:, a * NE:(a + 1) * NE], tri[:, 1, :], msum[:, par, a, :], start=False, stop=True)
            mm.then_inc(rank_mm, 1)

        eng.wait_ge(c_col_done, 2)
        eng.wait_ge(wm_ld[0], 16)
        modulation(0, SB[0])
        eng.wait_ge(k_ld, 64)
        transpose_h1(-1, X, (1,))
        transpose_h1(0, Y, (0, 1))
        eng.wait_ge(w_lo, 1)
        eng.wait_ge(hT_lo, 1)
        project_qk(0, 0)
        for j in range(2):
            eng.wait_ge(qk_lo, 3 + j)
            project_v(j, j, 0, (X, Y)[j])
        eng.wait_ge(wm_ld[1], 16)
        modulation(1, SB[1])
        modulation(2, TB[0])
        eng.wait_ge(cst, 9)
        eng.wait_ge(qk_ld, LD)
        eng.wait_ge(mod_cp, 4)
        eng.wait_ge(gate_dve, 10)
        for q in range(4):
            scores(0, 0, 0, q)
        eng.wait_ge(v_ev, 1)
        transpose_max(0, 0, X)
        eng.wait_ge(w_lo, 2)

        def tile(n, t, e, i):
            j, par, p2 = t % 2, (t // 2) % 2, t % 2
            m, tm = n - 1, (t - 1) % 4
            n1, j1, par1 = n + 1, (t + 1) % 2, ((t + 1) // 2) % 2
            if runs(n, 1):
                if j == 0:
                    eng.wait_ge(h2T_lo, n - 1)
                else:
                    eng.wait_ge(mt_cp, n + 1)
                transpose_o(m, X)
            if j == 0 and runs(n, 0, TILES - 3):
                eng.wait_ge(mt_cp, n + 1)
                if isinstance(n, int) and n == 0:
                    eng.wait_ge(v_ev, 2)
                transpose_h1(e + 1, Y, (0, 1))
                if runs(n, 1):
                    eng.wait_ge(oT_lo, m + 1)
                project_qk(e + 1, (t // 2 + 1) % 2)
            if j == 1 and runs(n, 0, TILES - 2):
                eng.wait_ge(qk_lo, 4 * e + 8)
                if runs(n, 2):
                    eng.wait_ge(h2T_lo, n - 1)
                project_v(n + 1, 0, (t // 2 + 1) % 2, Y)
                eng.wait_ge(oT_lo, m + 1)
                project_v(n + 2, 1, (t // 2 + 1) % 2, X)
            if runs(n, 1):
                if j == 0 and runs(n, 0, TILES - 3):
                    eng.wait_ge(qk_lo, 4 * e + 7)
                if j == 1:
                    if runs(n, 0, TILES - 2):
                        eng.wait_ge(v_ev, n + 2)
                    else:
                        eng.wait_ge(h2T_lo, n - 1)
                project_out(m, (X, Y)[j])
            if j == 1 and runs(n, 3):
                if runs(n, 0, TILES - 2):
                    eng.wait_ge(v_ev, n + 3)
                else:
                    eng.wait_ge(oT_lo, m + 1)
                router(e - 1, (t - 3) % 4, X)
            if j == 0 and runs(n, 4):
                if runs(n, 0, TILES - 3):
                    eng.wait_ge(qk_lo, 4 * e + 8)
                else:
                    eng.wait_ge(mt_cp, n + 1)
                ranks(e - 2, par, Y)
            if runs(n, 0, TILES - 2):
                eng.wait_ge(qk_ld, LD * (e + j + 1))
            eng.wait_ge(mm_ld[p2], 16 * e + 16)
            eng.wait_ge(v_ev, n + 1)
            for q in range(4):
                if runs(n, 0, TILES - 2):
                    scores(n1, j1, par1, q)
                scores_t(n, j, par, p2, q)
                if q == 1 and runs(n, 1):
                    eng.wait_ge(nrm, 3 * n)
                if q >= 1:
                    weigh(n, t, q - 1)
            weigh(n, t, 3)
            if runs(n, 0, TILES - 2):
                if runs(n, 1):
                    eng.wait_ge(ln2_dve, L2_OPS * m + 1)
                else:
                    eng.wait_ge(qk_lo, 8)
                transpose_max(n1, (t + 1) % 2, (X, Y)[j])
            if runs(n, 1):
                if j == 0:
                    if runs(n, 4):
                        eng.wait_ge(p_dve, P_OPS * (e - 2) + 1)
                    else:
                        eng.wait_ge(qk_lo, 4 * e + 8)
                else:
                    if runs(n, 3):
                        eng.wait_ge(r_dve, R_OPS * (e - 1) + 4)
                    else:
                        eng.wait_ge(v_ev, n + 3)
                transpose_h2(m, tm, (Y, X)[j])

        for_tiles(eng, tile)
        m = TILES - 1
        eng.wait_ge(ln2_dve, L2_OPS * (m - 1) + 1)
        transpose_o(m, Y)
        eng.wait_ge(h2T_lo, m)
        project_out(m, X)
        eng.wait_ge(oT_lo, m + 1)
        ranks(GROUPS - 2, 0, Y)
        eng.wait_ge(ln2_dve, L2_OPS * m + 1)
        transpose_h2(m, 3, X)
        eng.wait_ge(p_dve, P_OPS * (GROUPS - 2) + 1)
        router(GROUPS - 1, 2, Y)
        ranks(GROUPS - 1, 1, X)
        eng.wait_ge(r_dve, R_OPS * (GROUPS - 1) + 4)
        eng.matmul(Y[:, 0:NE], tri[:, 1, :], msum[:, 0, 0, :], start=True, stop=True).then_inc(cnt_mm, 1)


def experts_and_output(nc, A, T, out, ctx, own):

    def sb(name, shape, dt=F32):
        return ctx.enter_context(nc.sbuf_tensor(name, shape, dt))

    def pb(name, shape):
        return ctx.enter_context(nc.psum_tensor(name, shape, F32))

    def sem(name):
        return own.enter_context(nc.semaphore(name))

    def sems(name, n):
        return [sem(f"{name}{i}") for i in range(n)]

    ident, iota_e, pack, count, gb = T["ident"], T["iota_e"], T["pack"], T["count"], T["gb"]
    xs, ys = T["xs_scr"], T["ys_scr"]
    NS = STEPS_RUN

    gu_raw = sb("gu_raw", [P, NE, KD, 2 * FI])
    dn_raw = sb("dn_raw", [FH, NE, 2, D])
    gu_hl = sb("gu_hl", [P, RING, KD, 2, 2 * FI], F32R)
    dn_hl = sb("dn_hl", [FH, RING, 2, 2, D], F32R)
    sgu_raw = sb("sgu_raw", [P, KD, 2, SH_I])
    sdn_raw = sb("sdn_raw", [FH, 4, D])
    sgu_hl = sb("sgu_hl", [P, KD, 2, 2, SH_I], F32R)
    sdn_hl = sb("sdn_hl", [FH, 4, 2, D], F32R)

    steps_c = sb("steps_c", [P, 1 + 2 * NE])
    tab = sb("tab", [P, 8, NE])
    tab2 = sb("tab2", [P, 2, NE, NE])
    col = sb("col", [P, 8])
    pad_i = sb("pad_i", [P, 2, NE], I32)
    step_i = sb("step_i", [1, 3, P], I32)
    g_oh = sb("g_oh", [P, TILES, TOPK, NE])
    g_sh = sb("g_sh", [P, TILES, TOPK])
    g_row = sb("g_row", [P, TILES, TOPK])
    g_idx = sb("g_idx", [P, TILES, TOPK], U32)

    x_st = sb("x_st", [P, 4, D])
    xT = sb("xT", [P, 2, 2, KD, P], F32R)
    g_act = sb("g_act", [P, 2, SH_I])
    h_act = sb("h_act", [P, 2, SH_I])
    aT = sb("aT", [FH, 2, 2, 4, P], F32R)
    y_st = sb("y_st", [P, 4, D])
    x1_in = sb("x1_in", [P, 2, D])
    z_in = sb("z_in", [P, 2, D])
    y_in = sb("y_in", [P, 2, TOPK, D])
    o_st = sb("o_st", [P, 2, D])
    w_now = sb("w_now", [P, 2, TOPK])
    idx_now = sb("idx_now", [P, 2, TOPK], U32)

    XT = [pb(f"XT{i}", [P, 512]) for i in range(2)]
    GU = [pb(f"GU{i}", [P, 512]) for i in range(2)]
    HT = [pb(f"HT{i}", [P, 512]) for i in range(2)]
    YP = [pb(f"YP{i}", [P, 512]) for i in range(2)]

    cst_ld, sh_ld, wq_ld = sem("cst_ld"), sem("sh_ld"), sems("wq_ld", 4)
    tb, col_mm, step_tab, g_tab = sem("tb"), sem("col_mm"), sem("step_tab"), sem("g_tab")
    pad_st, w_split, sh_split = sem("pad_st"), sem("w_split"), sem("sh_split")
    xs_ld = sems("xs_ld", 4)
    xt_mm, xT_hi2, xT_lo2 = sem("xt_mm"), sem("xT_hi2"), sem("xT_lo2")
    gu_mm, silu, gated = sem("gu_mm"), sem("silu"), sem("gated")
    ht_mm, aT_hi, aT_lo = sem("ht_mm"), sem("aT_hi"), sem("aT_lo")
    y_mm, y_out = sem("y_mm"), sem("y_out")
    ys_st = sems("ys_st", 4)
    x1_ld, y_gt, fin_dve, o_out = sems("x1_ld", 2), sems("y_gt", 2), sem("fin_dve"), sems("o_out", 2)
    w_cp, idx_cp = sem("w_cp"), sem("idx_cp")
    block = ctx.enter_context(nc.Block())

    def three(eng, dst, pairs):
        for i, (l_hi, l_lo, r_hi, r_lo) in enumerate(pairs):
            for j, (a, b) in enumerate(((l_hi, r_hi), (l_lo, r_hi), (l_hi, r_lo))):
                mm = eng.matmul(dst, a, b, start=(i + j == 0), stop=(i == len(pairs) - 1 and j == 2))
        return mm

    ITEMS = NS + TILES

    @block.sync
    def _(eng):
        eng.dma_start(steps_c[:, :], A["steps"]).then_inc(cst_ld, 16)
        eng.wait_ge(tb, TB_PAD)
        with eng.Fori(0, NE // 4) as i:
            for e in range(4):
                row = eng.value_load(pad_i[0:1, 0, bass.ds(4 * i + e, 1)], min_val=0, max_val=NE * CAP)
                eng.dma_start(xs[bass.ds(row, P), :], T["zeros"][:, :]).then_inc(pad_st, 16)
        eng.wait_ge(step_tab, 1)
        eng.wait_ge(pad_st, 16 * NE)

        def load_x(w, t):
            if runs(w, 4):
                eng.wait_ge(xt_mm, w - 3)
            row = eng.value_load(step_i[0:1, 0, bass.ds(w, 1)], min_val=0, max_val=NE * CAP)
            eng.dma_start(x_st[:, t, :], xs[bass.ds(row, P), :]).then_inc(xs_ld[t], 16)

        def store_y(w, t):
            eng.wait_ge(y_out, w + 1)
            plain(eng)
            eng.dma_start(ys[bass.ds(P * w, P), :], y_st[:, t, :]).then_inc(ys_st[t], 16)

        for t in range(4):
            load_x(t, t)

        def step(w, t, i):
            if runs(w, 2):
                store_y(w - 2, (t - 2) % 4)
            if runs(w, 0, NS - 5):
                load_x(w + 4, t)
            else:
                load_h2(w + 4 - NS, t)

        def load_h2(n, t):
            eng.wait_ge(xt_mm, NS + n - 3)
            plain(eng)
            eng.dma_start(x_st[:, t, :], T["h2_scr"][n]).then_inc(xs_ld[t], 16)

        for_steps(eng, step, NS)
        store_y(NS - 2, 2)
        store_y(NS - 1, 3)

        def load_x1(n, t):
            if runs(n, 2):
                eng.wait_ge(fin_dve, FIN * (n - 2) + 1)
                plain(eng)
            eng.dma_start(x1_in[:, t % 2, :], T["x1_scr"][n]).then_inc(x1_ld[t % 2], 16)

        def store_out(n, t):
            eng.wait_ge(fin_dve, FIN * (n + 1))
            plain(eng)
            for c in range(2):
                eng.dma_start(out.rearrange("(c n q) d -> n c q d", c=2, n=TILES)[n, c],
                              o_st[c * CH:(c + 1) * CH, t % 2, :]).then_inc(o_out[t % 2], 16)

        load_x1(0, 0)

        def tile(n, t, e, i):
            if runs(n, 0, TILES - 2):
                load_x1(n + 1, (t + 1) % 4)
            if runs(n, 0, TILES - 5):
                load_h2(n + 4, t)
            if runs(n, 1):
                store_out(n - 1, (t - 1) % 4)

        for_tiles(eng, tile)
        store_out(TILES - 1, 3)
        for t in range(2):
            eng.wait_ge(o_out[t], 32 * (TILES // 2))
        for t in range(4):
            eng.wait_ge(ys_st[t], 16 * (NS // 4))
        eng.wait_ge(pad_st, 16 * NE)

    @block.scalar
    def _(eng):
        for q in range(4):
            e = slice(4 * q, 4 * q + 4)
            eng.dma_start(gu_raw[:, e], A["egu"][:, e]).then_inc(wq_ld[q], 16)
            eng.dma_start(dn_raw[:, e], A["ed"][:, e]).then_inc(wq_ld[q], 16)
            if q == 1:
                eng.dma_start(sgu_raw[:, :, :, :], A["sgu"]).then_inc(sh_ld, 16)
                eng.dma_start(sdn_raw[:, :, :], A["sd"]).then_inc(sh_ld, 16)

        def x_hi(w, p2):
            eng.wait_ge(xt_mm, w + 1)
            if runs(w, 2):
                eng.wait_ge(gu_mm, w - 1)
            eng.activation(xT[:, p2, 0, :, :], XT[p2][:, 0:D].rearrange("p (k x) -> p k x", k=KD), ACT.Copy).then_inc(xT_hi2, 1)

        def a_hi(w, p2, k, counts=1):
            eng.wait_ge(ht_mm, w + 1)
            eng.activation(aT[:, p2, 0, 0:k, :], HT[p2][0:FH, 0:k * P].rearrange("p (k x) -> p k x", k=k), ACT.Copy).then_inc(aT_hi, 1)

        x_hi(0, 0)

        def step(w, t, i):
            p2 = t % 2
            eng.wait_ge(gu_mm, w + 1)
            if runs(w, 2):
                eng.wait_ge(gated, w - 1)
            eng.activation(g_act[:, p2, 0:FI], GU[p2][:, 0:FI], ACT.Silu).then_inc(silu, 1)
            x_hi(w + 1, 1 - p2)
            if runs(w, 2):
                eng.wait_ge(y_mm, w - 1)
            a_hi(w, p2, 2)

        for_steps(eng, step, NS)

        def tile(n, t, e, i):
            w, p2 = NS + n, t % 2
            eng.wait_ge(gu_mm, w + 1)
            eng.wait_ge(gated, w - 1)
            eng.activation(g_act[:, p2, :], GU[0][:, 0:SH_I], ACT.Silu).then_inc(silu, 1)
            if runs(n, 0, TILES - 2):
                x_hi(w + 1, 1 - p2)
            eng.wait_ge(y_mm, w - 1)
            a_hi(w, p2, 4)

        for_tiles(eng, tile)

    @block.gpsimd
    def _(eng):
        def split_lo(e, r, raw_g, raw_d):
            eng.tensor_tensor(gu_hl[:, r, :, 1, :], raw_g, gu_hl[:, r, :, 0, :].bitcast(F32), ALU.subtract).then_inc(w_split, 1)
            eng.tensor_tensor(dn_hl[:, r, :, 1, :], raw_d, dn_hl[:, r, :, 0, :].bitcast(F32), ALU.subtract).then_inc(w_split, 1)

        def expert(e, r, raw_g, raw_d):
            eng.tensor_copy(gu_hl[:, r, :, 0, :], raw_g).then_inc(w_split, 1)
            eng.tensor_copy(dn_hl[:, r, :, 0, :], raw_d).then_inc(w_split, 1)
            eng.wait_ge(w_split, 4 * e + 2)
            if not isinstance(e, int):
                plain(eng)
            split_lo(e, r, raw_g, raw_d)

        for r in range(RING):
            eng.wait_ge(wq_ld[0], 32)
            expert(r, r, gu_raw[:, r], dn_raw[:, r])
        eng.wait_ge(tb, TB_PAD)
        for q in range(1, NE // RING):
            eng.wait_ge(wq_ld[q], 32)
        with eng.Fori(1, NE // RING) as i:
            for r in range(RING):
                e = RING * i + r
                last = eng.value_load(pad_i[0:1, 1, bass.ds(e - RING, 1)], min_val=0, max_val=NS)
                eng.wait_ge(y_mm, last)
                plain(eng)
                expert(e, r, gu_raw[:, bass.ds(e, 1)].rearrange("p e k x -> p (e k) x"),
                       dn_raw[:, bass.ds(e, 1)].rearrange("p e k x -> p (e k) x"))

        eng.wait_ge(g_tab, 1)
        for t in range(4):
            eng.wait_ge(ys_st[t], 16 * (NS // 4))

        def tile(n, t, e, i):
            if runs(n, 2):
                eng.wait_ge(fin_dve, FIN * (n - 1))
                plain(eng)
            eng.tensor_copy(idx_now[:, t % 2, :], g_idx[:, bass.ds(n, 1), :].rearrange("p o k -> p (o k)")).then_inc(idx_cp, 1)
            eng.wait_ge(idx_cp, n + 1)
            plain(eng)
            for k in range(TOPK):
                eng.indirect_dma_start(y_in[:, t % 2, k, :], None, ys,
                                       bass.IndirectOffsetOnAxis(ap=idx_now[:, t % 2, k:k + 1], axis=0)).then_inc(y_gt[t % 2], 16)

        for_tiles(eng, tile)

    @block.vector
    def _(eng):
        c = Chain(eng, tb, 0)

        def row(i):
            return tab[:, i, :]

        n_t, cum, before, shift, pads = row(0), row(1), row(2), row(3), row(4)
        eng.wait_ge(cst_ld, 16)
        j128, ringw, part = steps_c[:, 1:1 + NE], steps_c[:, 1 + NE:1 + 2 * NE], steps_c[:, 0:1]
        e_row, e_cap = iota_e[:, 0, :], iota_e[:, 1, :]

        def over(ap, outer):
            return (ap.unsqueeze(2) if outer else ap.unsqueeze(1)).broadcast_to([P, NE, NE])

        c.mark(eng.tensor_tensor(tab2[:, 0], over(count[:, :], True), over(j128, False), ALU.is_gt)).wait()
        c.mark(eng.tensor_reduce(n_t, tab2[:, 0], AX.X, ALU.add))
        c.mark(eng.tensor_tensor(tab2[:, 1], over(e_row, False), over(e_row, True), ALU.is_le)).wait()
        c.mark(eng.tensor_tensor(tab2[:, 0], tab2[:, 1], over(n_t, False), ALU.mult)).wait()
        c.mark(eng.tensor_reduce(cum, tab2[:, 0], AX.X, ALU.add)).wait()
        c.mark(eng.tensor_tensor(before, cum, n_t, ALU.subtract))
        c.mark(eng.tensor_tensor(pads, e_cap, count[:, :], ALU.add)).wait()
        c.mark(eng.tensor_copy(pad_i[:, 0, :], pads))
        c.mark(eng.tensor_scalar(pad_i[:, 1, :], cum, 1.0, None, ALU.max))
        assert c.k == TB_PAD
        c.mark(eng.scalar_tensor_tensor(out=shift, in0=before, scalar=-float(P), in1=e_cap, op0=ALU.mult, op1=ALU.add))
        c.mark(eng.tensor_scalar(row(5), cum, part, None, ALU.is_le)).wait()
        c.mark(eng.tensor_reduce(col[:, 0:1], row(5), AX.X, ALU.add))
        c.mark(eng.tensor_tensor(row(6), row(5), ringw, ALU.mult)).wait()
        c.mark(eng.tensor_reduce(col[:, 2:3], row(6), AX.X, ALU.add))
        c.mark(eng.tensor_scalar(row(7), e_row, col[:, 0:1], None, ALU.is_equal)).wait()
        c.mark(eng.tensor_tensor(row(6), row(7), shift, ALU.mult)).wait()
        c.mark(eng.tensor_reduce(col[:, 4:5], row(6), AX.X, ALU.add)).wait()
        c.mark(eng.scalar_tensor_tensor(out=col[:, 5:6], in0=part, scalar=float(P), in1=col[:, 4:5], op0=ALU.mult, op1=ALU.add))
        c.mark(eng.tensor_scalar(col[:, 6:7], col[:, 0:1], float(NE), float(NE * CAP), ALU.is_ge, ALU.mult)).wait()
        c.mark(eng.tensor_tensor(col[:, 7:8], col[:, 5:6], col[:, 6:7], ALU.add)).wait()
        c.mark(eng.tensor_scalar(col[:, 1:2], col[:, 7:8], float(NE * CAP), None, ALU.min))
        c.mark(eng.tensor_scalar(col[:, 3:4], col[:, 0:1], 1.0, float(NE), ALU.add, ALU.min))
        assert c.k == TB_COL
        eng.wait_ge(col_mm, 1)
        eng.tensor_copy(step_i[:, :, :], YP[0][0:1, 0:3 * P].rearrange("p (a x) -> p a x", a=3)).then_inc(step_tab, 1)
        c.mark(eng.tensor_tensor(g_oh[:, :, :, :], pack[:, :, 0:TOPK].unsqueeze(3).broadcast_to([P, TILES, TOPK, NE]),
                                 e_row.unsqueeze(1).unsqueeze(1).broadcast_to([P, TILES, TOPK, NE]), ALU.is_equal)).wait()
        c.mark(eng.tensor_tensor(g_oh[:, :, :, :], g_oh[:, :, :, :],
                                 shift.unsqueeze(1).unsqueeze(1).broadcast_to([P, TILES, TOPK, NE]), ALU.mult)).wait()
        c.mark(eng.tensor_reduce(g_sh[:, :, :], g_oh[:, :, :, :], AX.X, ALU.add)).wait()
        c.mark(eng.tensor_tensor(g_row[:, :, :], pack[:, :, TOPK:2 * TOPK], g_sh[:, :, :], ALU.subtract)).wait()
        eng.tensor_copy(g_idx[:, :, :], g_row[:, :, :]).then_inc(g_tab, 1)

        def x_lo(w, p2):
            eng.wait_ge(xT_hi2, w + 1)
            eng.tensor_tensor(xT[:, p2, 1, :, :], XT[p2][:, 0:D].rearrange("p (k x) -> p k x", k=KD),
                              xT[:, p2, 0, :, :].bitcast(F32), ALU.subtract).then_inc(xT_lo2, 1)

        def a_lo(w, p2, k):
            eng.wait_ge(aT_hi, w + 1)
            eng.tensor_tensor(aT[:, p2, 1, 0:k, :], HT[p2][0:FH, 0:k * P].rearrange("p (k x) -> p k x", k=k),
                              aT[:, p2, 0, 0:k, :].bitcast(F32), ALU.subtract).then_inc(aT_lo, 1)

        def y_gate(w, t, i):
            eng.wait_ge(y_mm, w + 1)
            if runs(w, 4):
                eng.wait_ge(ys_st[t], 16 * i)
            eng.tensor_tensor(y_st[:, t, :], YP[t % 2][:, 0:D], gb[:, :], ALU.mult).then_inc(y_out, 1)

        x_lo(0, 0)

        def step(w, t, i):
            p2 = t % 2
            eng.wait_ge(silu, w + 1)
            if runs(w, 2):
                eng.wait_ge(ht_mm, w - 1)
            eng.tensor_tensor(h_act[:, p2, 0:FI], GU[p2][:, FI:2 * FI], g_act[:, p2, 0:FI], ALU.mult).then_inc(gated, 1)
            x_lo(w + 1, 1 - p2)
            if runs(w, 1):
                y_gate(w - 1, (t - 1) % 4, i if t else i - 1)
            a_lo(w, p2, 2)

        for_steps(eng, step, NS)
        y_gate(NS - 1, 3, NS // 4 - 1)
        eng.wait_ge(sh_ld, 32)
        c2 = Chain(eng, sh_split, 0)
        c2.mark(eng.tensor_copy(sgu_hl[:, :, 0, :, :], sgu_raw[:, :, :, :]))
        c2.mark(eng.tensor_tensor(sdn_raw[:, :, :], sdn_raw[:, :, :], gb[0:FH, :].unsqueeze(1).broadcast_to([FH, 4, D]),
                                  ALU.mult)).wait()
        c2.mark(eng.tensor_copy(sdn_hl[:, :, 0, :], sdn_raw[:, :, :]))
        c2.mark(eng.tensor_tensor(sgu_hl[:, :, 1, :, :], sgu_raw[:, :, :, :], sgu_hl[:, :, 0, :, :].bitcast(F32),
                                  ALU.subtract)).wait()
        c2.mark(eng.tensor_tensor(sdn_hl[:, :, 1, :], sdn_raw[:, :, :], sdn_hl[:, :, 0, :].bitcast(F32), ALU.subtract))
        assert c2.k == SH_OPS

        def finish(n, t, i2):
            p2 = t % 2
            c = Chain(eng, fin_dve, FIN * n)
            eng.wait_ge(y_mm, NS + n + 1)
            eng.wait_ge(x1_ld[p2], 16 * i2 + 16)
            c.mark(eng.tensor_tensor(z_in[:, p2, :], YP[p2][:, 0:D], x1_in[:, p2, :], ALU.add)).wait()
            eng.wait_ge(y_gt[p2], 16 * TOPK * (i2 + 1))
            acc = z_in[:, p2, :]
            for k in range(TOPK):
                if k == TOPK - 1 and runs(n, 2):
                    eng.wait_ge(o_out[p2], 32 * i2)
                to = o_st[:, p2, :] if k == TOPK - 1 else z_in[:, p2, :]
                c.mark(eng.scalar_tensor_tensor(out=to, in0=y_in[:, p2, k, :], scalar=w_now[:, p2, k:k + 1],
                                                in1=acc, op0=ALU.mult, op1=ALU.add))
                if k < TOPK - 1:
                    c.wait()
            assert c.k == FIN

        def weights(n, p2):
            eng.tensor_scalar(w_now[:, p2, :], pack[:, bass.ds(n, 1), 2 * TOPK:3 * TOPK].rearrange("p o k -> p (o k)"), 1.0,
                              None, ALU.mult).then_inc(w_cp, 1)

        def tile(n, t, e, i):
            w, p2 = NS + n, t % 2
            eng.wait_ge(silu, w + 1)
            eng.wait_ge(ht_mm, w - 1)
            eng.tensor_tensor(h_act[:, p2, :], GU[1][:, 0:SH_I], g_act[:, p2, :], ALU.mult).then_inc(gated, 1)
            if runs(n, 0, TILES - 2):
                x_lo(w + 1, 1 - p2)
            a_lo(w, p2, 4)
            if runs(n, 1):
                finish_prev(n, t, e, i)

        def finish_prev(n, t, e, i):
            m = n - 1
            weights(m, (t - 1) % 2)
            eng.wait_ge(w_cp, n)
            finish(m, (t - 1) % 4, e - (0 if t % 2 else 1))

        for_tiles(eng, tile)
        weights(TILES - 1, 1)
        eng.wait_ge(w_cp, TILES)
        finish(TILES - 1, 3, GROUPS - 1)

    @block.tensor
    def _(eng):
        eng.wait_ge(tb, TB_COL)
        for a in range(3):
            mm = eng.matmul(YP[0][0:1, a * P:(a + 1) * P], col[:, a + 1:a + 2], ident[:, :], start=True, stop=True)
        mm.then_inc(col_mm, 1)
        eng.wait_ge(step_tab, 1)

        def transpose_x(w, t, count):
            eng.wait_ge(xs_ld[t], 16 * count)
            if runs(w, 2):
                eng.wait_ge(xT_lo2, w - 1)
            for k in range(KD):
                mm = eng.transpose(XT[t % 2][:, k * P:(k + 1) * P], x_st[:, t, k * P:(k + 1) * P], ident[:, :])
            mm.then_inc(xt_mm, 1)

        def x_pairs(p2, k):
            return xT[:, p2, 0, k, :], xT[:, p2, 1, k, :]

        def gate_up(w, t, slot, need):
            p2 = t % 2
            eng.wait_ge(w_split, need)
            eng.wait_ge(xT_lo2, w + 1)
            if runs(w, 2):
                eng.wait_ge(gated, w - 1)
            three(eng, GU[p2][:, 0:2 * FI],
                  [x_pairs(p2, k) + tuple(gu_hl[:, bass.ds(slot, 1), k, hl, :].rearrange("p o x -> p (o x)") for hl in range(2))
                   for k in range(KD)]).then_inc(gu_mm, 1)

        def transpose_a(w, t, tiles):
            p2 = t % 2
            eng.wait_ge(gated, w + 1)
            if runs(w, 2):
                eng.wait_ge(aT_lo, w - 1)
            for k in range(tiles):
                mm = eng.transpose(HT[p2][0:FH, k * P:(k + 1) * P], h_act[:, p2, k * FH:(k + 1) * FH], ident[:, :])
            mm.then_inc(ht_mm, 1)

        def down(w, t, slot):
            p2 = t % 2
            eng.wait_ge(aT_lo, w + 1)
            if runs(w, 2):
                eng.wait_ge(y_out, w - 1)
            three(eng, YP[p2][:, 0:D],
                  [(aT[:, p2, 0, k, :], aT[:, p2, 1, k, :]) +
                   tuple(dn_hl[:, bass.ds(slot, 1), k, hl, :].rearrange("p o x -> p (o x)") for hl in range(2))
                   for k in range(2)]).then_inc(y_mm, 1)

        def load_entry(a, w, most):
            return eng.value_load(step_i[0:1, a, bass.ds(w, 1)], min_val=0, max_val=most)

        transpose_x(0, 0, 1)

        def step(w, t, i):
            need = load_entry(2, w, NE)
            slot = load_entry(1, w, RING - 1)
            gate_up(w, t, slot, 4 * need)
            transpose_x(w + 1, (t + 1) % 4, (i + 1) + (1 if t == 3 else 0))
            if runs(w, 1):
                down(w - 1, (t - 1) % 4, load_entry(1, w - 1, RING - 1))
            transpose_a(w, t, 2)

        for_steps(eng, step, NS)
        down(NS - 1, 3, load_entry(1, NS - 1, RING - 1))
        eng.wait_ge(sh_split, SH_OPS)

        def shared_down(n, t):
            w, p2 = NS + n, t % 2
            eng.wait_ge(aT_lo, w + 1)
            if runs(n, 2):
                eng.wait_ge(fin_dve, FIN * (n - 2) + 1)
            else:
                eng.wait_ge(y_out, w - 1)
            three(eng, YP[p2][:, 0:D], [(aT[:, p2, 0, k, :], aT[:, p2, 1, k, :], sdn_hl[:, k, 0, :], sdn_hl[:, k, 1, :])
                                        for k in range(4)]).then_inc(y_mm, 1)

        def tile(n, t, e, i):
            w, p2 = NS + n, t % 2
            eng.wait_ge(xT_lo2, w + 1)
            eng.wait_ge(gated, w)
            for u in range(2):
                mm = three(eng, GU[u][:, 0:SH_I], [x_pairs(p2, k) + (sgu_hl[:, k, 0, u, :], sgu_hl[:, k, 1, u, :]) for k in range(KD)])
            mm.then_inc(gu_mm, 1)
            if runs(n, 0, TILES - 2):
                transpose_x(w + 1, (t + 1) % 4, NS // 4 + (i + 1) + (1 if t == 3 else 0))
            if runs(n, 1):
                shared_down(n - 1, (t - 1) % 4)
            transpose_a(w, t, 4)

        for_tiles(eng, tile)
        shared_down(TILES - 1, 3)


def program(nc, A, out):
    with ExitStack() as keep:
        T = {}
        for name, shape in (("q_scr", (GROUPS, 2, 2, P, 2 * P)), ("k_scr", (GROUPS, 2, 2, P, 2 * WIN)),
                            ("kv_scr", (GROUPS, HEADS, WIN)), ("x1_scr", (TILES, P, D)), ("h2_scr", (TILES, P, D)),
                            ("xs_scr", (NE * CAP + P, D)), ("ys_scr", (STEPS_RUN * P, D))):
            T[name] = nc.dram_tensor(name, shape, F32).ap()
        for name, shape in (("ident", [P, P]), ("iota_e", [P, 2, NE]), ("gb", [P, D]), ("pack", [P, TILES, 3 * TOPK]),
                            ("count", [P, NE]), ("zeros", [P, D])):
            T[name] = keep.enter_context(nc.sbuf_tensor(name, shape, F32))
        with ExitStack() as ctx:
            attention_and_routing(nc, A, T, ctx, keep)
        with ExitStack() as ctx:
            experts_and_output(nc, A, T, out, ctx, keep)


def constants():
    import numpy as np

    q, r = np.arange(CH), np.arange(CH - 1)
    masks = np.zeros((MASKS + 1, 2, P), np.float32)
    masks[r, 0, r] = 1
    masks[CH - 1 + r, 0, CH + 1 + r] = 1
    masks[MASKS, 0, :] = 1
    hidden = np.concatenate([q[None, :] > r[:, None], q[None, :] <= r[:, None]], 0)
    masks[:MASKS, 1, :] = np.where(np.concatenate([hidden, hidden], 1), -BIG, 0.0)
    tris = np.zeros((P, 2, P), np.float32)
    tris[:, 0, :] = np.triu(np.ones((P, P)), 1)
    tris[:, 1, :] = 1
    e = np.arange(NE, dtype=np.float32)
    iotas = np.broadcast_to(np.stack([e, e * CAP]), (P, 2, NE))
    ring = np.where(np.arange(NE) % RING == RING - 1, 1 - RING, 1)
    steps = np.concatenate([np.arange(P)[:, None], np.tile(P * e, (P, 1)), np.tile(ring, (P, 1))], 1)
    return {"steps": steps.astype(np.float32), "ident": np.eye(P, dtype=np.float32), "masks": masks, "tris": tris,
            "iotas": np.ascontiguousarray(iotas, dtype=np.float32)}


def host_layout(x):
    import numpy as np

    def cols(w, kp):
        w = np.asarray(w)
        return np.ascontiguousarray(w.T.reshape(-1, kp, w.shape[0]).transpose(1, 0, 2))

    g = {k.replace("L0_ffn_", "").replace("L0_attn_", "").replace("L0_", ""): np.asarray(v) for k, v in x.items()}
    w = g["w_qkv"]
    a = {"x": g["x"][0], "c": np.ascontiguousarray(g["c"].reshape(KD, P).T),
         "wmod": np.ascontiguousarray(g["wmod"].reshape(KD, P, 6 * D).transpose(1, 0, 2)),
         "wq": cols(w[0:D], P), "wk": cols(w[D:2 * D], P), "wv": cols(w[2 * D:], P), "wo": cols(g["w_out"], P),
         "rg": cols(g["rg_w"], P), "ru": cols(g["ru_w"], P), "escale": g["extra_scale"], "ebias": g["extra_bias"],
         "egu": np.ascontiguousarray(np.concatenate([g["Wg"], g["Wu"]], 1).reshape(NE, 2 * FI, KD, P).transpose(3, 0, 2, 1)),
         "ed": np.ascontiguousarray(g["Wd"].reshape(NE, D, 2, FH).transpose(3, 0, 2, 1)),
         "sgu": np.ascontiguousarray(np.stack([g["Sg"], g["Su"]]).reshape(2, SH_I, KD, P).transpose(3, 2, 0, 1)),
         "sd": cols(g["Sd"], FH)}
    return a | constants()


def kernel(**inputs):
    import numpy as np
    import concourse.bacc as bacc
    from concourse.bass_utils import run_bass_kernel_spmd

    nc = bacc.Bacc("TRN2", target_bir_lowering=False, num_devices=1)
    arrays = {f"in_{name}": a for name, a in host_layout(inputs).items()}
    A = {name[3:]: nc.dram_tensor(name, a.shape, mybir.dt.from_np(a.dtype), kind="ExternalInput").ap()
         for name, a in arrays.items()}
    out = nc.dram_tensor("out_x", (S_LEN, D), F32, kind="ExternalOutput").ap()
    program(nc, A, out)
    result = run_bass_kernel_spmd(nc, [arrays], core_ids=[0])
    return np.asarray(result.results[0]["out_x"]).reshape(1, S_LEN, D)
```

```python
from contextlib import ExitStack

import concourse.bass as bass
from concourse import mybir

P = 128
S_LEN, D = 2048, 256
HEADS, DH = 16, 16
CH = 64
KD = D // P
TILES = S_LEN // P
GROUPS = TILES // 2
NE, TOPK, FI = 16, 4, 176
FH = FI // 2
SH_I = 2 * FI
EPS = 1e-5
SCALE = 1.0 / DH ** 0.5
BIG = 2.0 ** 100
ROWS = 3 * DH
VALID = 2 * ROWS
MASKS = 2 * (CH - 1)
WIN = 3 * CH
CAP = S_LEN + P
STEPS = (S_LEN * TOPK + NE * (P - 1)) // P
ONE_V = 2 * DH
VC = ONE_V + 1
UNROLL = 24
STEPS_RUN = 8 + -(-(STEPS - 8) // UNROLL) * UNROLL
RING = 4
FIRST = 2 * RING
W_GU, W_DN = KD * 2 * FI, 2 * D
TB_PAD, TB_COL = 10, 25
SH_OPS, FIN = 5, 1 + TOPK
L1_OPS, L2_OPS = 16, 15
R_OPS, P_OPS = 24, 5
LD = 13 * 16

F32 = mybir.dt.float32
F32R = mybir.dt.float32r
U32 = mybir.dt.uint32
I32 = mybir.dt.int32
ALU = mybir.AluOpType
ACT = mybir.ActivationFunctionType
AX = mybir.AxisListType


def plain(eng):
    eng.nop(nofuse=True)


def for_tiles(eng, body):
    for t in range(4):
        body(t, t, t // 2, 0)
    with eng.Fori(1, TILES // 4 - 1) as i:
        for t in range(4):
            body(4 * i + t, t, 2 * i + t // 2, i)
    last = TILES // 4 - 1
    for t in range(4):
        body(4 * last + t, t, 2 * last + t // 2, last)


def for_steps(eng, body, count):
    for t in range(4):
        body(t, t, 0, t == 0, t == 3)
    with eng.Fori(0, (count - 8) // UNROLL) as j:
        for u in range(UNROLL):
            body(UNROLL * j + 4 + u, u % 4, UNROLL // 4 * j + 1 + u // 4, u == 0, u == UNROLL - 1)
    for t in range(4):
        body(count - 4 + t, t, count // 4 - 1, t == 0, t == 3)


def runs(n, low, high=None):
    return not isinstance(n, int) or (n >= low and (high is None or n <= high))


class Chain:

    def __init__(self, eng, sem, base):
        self.eng, self.sem, self.base, self.k = eng, sem, base, 0

    def mark(self, ins):
        ins.then_inc(self.sem, 1)
        self.k += 1
        return self

    def wait(self, is_plain=False):
        self.eng.wait_ge(self.sem, self.base + self.k)
        if is_plain:
            plain(self.eng)


def three(eng, out, pairs):
    for i, (l_hi, l_lo, r_hi, r_lo) in enumerate(pairs):
        for j, (a, b) in enumerate(((l_hi, r_hi), (l_lo, r_hi), (l_hi, r_lo))):
            mm = eng.matmul(out, a, b, start=(i + j == 0), stop=(i == len(pairs) - 1 and j == 2))
    return mm


def inverse_std(eng, ch, mv, nw, rs, nm):
    v, y, a, b = [nw[:, i, :] for i in range(4)]
    ch.mark(eng.tensor_scalar(v, mv[:, :, 1], EPS, None, ALU.add)).wait()
    ch.mark(eng.tensor_scalar(y.bitcast(I32), v.bitcast(I32), -0.5, float(0x5F3759DF), ALU.mult, ALU.add)).wait()
    for i in range(3):
        ch.mark(eng.scalar_tensor_tensor(out=a, in0=y, scalar=-0.5, in1=y, op0=ALU.mult, op1=ALU.mult)).wait()
        ch.mark(eng.tensor_tensor(b, a, v, ALU.mult)).wait()
        to = rs[:, :] if i == 2 else y
        ch.mark(eng.scalar_tensor_tensor(out=to, in0=b, scalar=1.5, in1=y, op0=ALU.add, op1=ALU.mult)).wait()
    ch.mark(eng.scalar_tensor_tensor(out=nm[:, :], in0=mv[:, :, 0], scalar=-1.0, in1=rs[:, :], op0=ALU.mult, op1=ALU.mult))


def load_stacked(eng, T, g, par, loaded, halves=(0, 1)):
    Q2, K2 = T["Q2"][par], T["K2"][par]
    for c in halves:
        for r in range(3):
            p0 = c * ROWS + r * DH
            q_rows = T["q_scr"][g, r % 2].rearrange("m j (h d) (c x) -> c d (m j h) x", d=DH, c=2)
            k_rows = T["k_scr"][g, r // 2].rearrange("m (h d) (c x) -> c d (m h) x", d=DH, c=2)
            eng.dma_start(Q2[p0:p0 + DH].rearrange("p m j h x -> p (m j h) x")[:, :, c * CH:(c + 1) * CH].bitcast(F32),
                          q_rows[c]).then_inc(loaded, 16)
            eng.dma_start(K2[p0:p0 + DH, :, :].bitcast(F32), k_rows[c]).then_inc(loaded, 16)
    if 1 in halves:
        eng.dma_start(K2[VALID:VALID + 1, :, :].bitcast(F32), T["kv_scr"][g]).then_inc(loaded, 16)


def send_rows(eng, T, t, par):
    for k in range(TOPK):
        eng.indirect_dma_start(T["xs_scr"], bass.IndirectOffsetOnAxis(ap=T["slot_u"][:, par, t % 2, k:k + 1], axis=0),
                               T["h2"][:, t, :], None).then_inc(T["disp"][t], 16)


def project_qkv(nc, A, T, ctx, own):

    def sb(name, shape, dt=F32):
        return ctx.enter_context(nc.sbuf_tensor(name, shape, dt))

    def pb(name, shape):
        return ctx.enter_context(nc.psum_tensor(name, shape, F32))

    def sem(name):
        return own.enter_context(nc.semaphore(name))

    def sems(name, n):
        return [sem(f"{name}{i}") for i in range(n)]

    ident, iota_e, mod, VW, Q2, K2, MM = [T[x] for x in ("ident", "iota_e", "mod", "VW", "Q2", "K2", "MM")]
    mask_key, mask_qry, tri, r_hl, esc, wo_hl = [T[x] for x in ("mask_key", "mask_qry", "tri", "r_hl", "esc", "wo_hl")]
    q_scr, k_scr = T["q_scr"], T["k_scr"]

    lent_used = [0]

    def lent(*shape):
        at, size = lent_used[0], shape[0] * shape[1] * (shape[2] if len(shape) > 2 else 1)
        lent_used[0] = at + size
        flat = T["lent"][:, at:at + size]
        return flat.rearrange("p (a b) -> p a b", a=shape[0]) if len(shape) == 2 else \
            flat.rearrange("p (a b c) -> p a b c", a=shape[0], b=shape[1])

    c_in = sb("c_in", [P, KD])
    c_tmp = sb("c_tmp", [P, 4, KD])
    c_col = sb("c_col", [P, KD, P])
    wmod = lent(KD, 6 * D)
    ones_f = sb("ones_f", [P, P])
    gate_a = sb("gate_a", [P, D])
    g_tmp = sb("g_tmp", [P, 3, D])
    w_raw = lent(KD, 4 * D)
    w_hl = sb("w_hl", [P, KD, 2, 3 * D], F32R)
    r_raw = sb("r_raw", [P, KD, 2 * NE])
    mk_raw = sb("mk_raw", [MASKS + 1, 2, P])
    tri_raw = sb("tri_raw", [P, 2, P])
    kval = sb("kval", [HEADS, 2, WIN], F32R)

    x_in = lent(2, 2, D)
    ln_st = sb("ln_st", [P, 2, 6])
    ln_mv = sb("ln_mv", [P, 2, 2])
    ln_nw = sb("ln_nw", [P, 4, 2])
    ln_rs = sb("ln_rs", [P, 2])
    ln_nm = sb("ln_nm", [P, 2])
    xn = lent(2, D)
    h_t = lent(2, D)
    h = lent(2, D)
    hT = sb("hT", [P, 2, KD, 2, 2, WIN], F32R)
    q_ev = sb("q_ev", [P, 2, 2, 2 * P], F32R)
    k_ev = sb("k_ev", [P, 2, 2, 2 * WIN], F32R)

    TH = [pb(f"TH{i}", [P, 512]) for i in range(2)]
    QB = [pb(f"QB{i}", [P, 512]) for i in range(4)]
    VB = [pb(f"VB{i}", [P, 512]) for i in range(2)]

    c_ld, wm_ld, w_ld, k_ld, e_ld = sem("c_ld"), sems("wm_ld", 2), sem("w_ld"), sem("k_ld"), sem("e_ld")
    c_exp, c_dve, c_col_done = sem("c_exp"), sem("c_dve"), sem("c_col_done")
    mod_mm, mod_cp, gate_dve = sem("mod_mm"), sem("mod_cp"), sem("gate_dve")
    w_hi, w_lo, wo_dve, wo_hi, wo_lo, cst = [sem(x) for x in ("w_hi", "w_lo", "wo_dve", "wo_hi", "wo_lo", "cst")]
    pre_pool, kv_st, z_set, z_st = sem("pre_pool"), sem("kv_st"), sem("z_set"), sem("z_st")
    xin_ld = sems("xin_ld", 2)
    ln1_dve, ln1_act, ln1_mod, h1_ready = [sem(x) for x in ("ln1_dve", "ln1_act", "ln1_mod", "h1_ready")]
    th1_mm, hT_hi, hT_lo, carry = sem("th1_mm"), sem("hT_hi"), sem("hT_lo"), sem("carry")
    qk_mm, qk_hi, qk_lo, qk_st, qk0_ld = [sem(x) for x in ("qk_mm", "qk_hi", "qk_lo", "qk_st", "qk0_ld")]
    v_mm, v_ev = sem("v_mm"), sem("v_ev")
    block = ctx.enter_context(nc.Block())
    x_t = A["x"].rearrange("(c n q) d -> n c q d", c=2, n=TILES)

    def for_groups(eng, body):
        body(0, 0, 0)
        with eng.Fori(0, GROUPS // 2 - 2) as i:
            body(2 * i + 1, 1, i)
            body(2 * i + 2, 0, i + 1)
        for g in range(GROUPS - 3, GROUPS):
            body(g, g % 2, g // 2)

    @block.sync
    def _(eng):
        eng.dma_start(c_in[:, :], A["c"]).then_inc(c_ld, 16)

        def load_in(tiles, par):
            for j, n in enumerate(tiles):
                for c in range(2):
                    src = x_t[n, c] if not isinstance(n, int) or n >= 0 else (A["x"][0:CH, :], x_t[TILES - 1, 0])[c]
                    eng.dma_start(x_in[c * CH:(c + 1) * CH, par, j, :], src).then_inc(xin_ld[par], 16)

        load_in((-1, -1), 1)
        eng.dma_start(wmod[:, :, 0:2 * D], A["wmod"][:, :, 0:2 * D]).then_inc(wm_ld[0], 16)
        load_in((0, 1), 0)
        eng.dma_start(ident[:, :], A["ident"]).then_inc(k_ld, 16)
        eng.dma_start(tri_raw[:, :, :], A["tris"]).then_inc(k_ld, 16)
        eng.dma_start(mk_raw[:, :, :], A["masks"]).then_inc(k_ld, 16)
        eng.dma_start(iota_e[:, :, :], A["iotas"]).then_inc(k_ld, 16)
        eng.wait_ge(ln1_act, 2)
        load_in((2, 3), 1)
        eng.wait_ge(ln1_act, 4)
        load_in((4, 5), 0)
        eng.wait_ge(pre_pool, 2)
        for g in range(GROUPS):
            eng.dma_start(T["kv_scr"][g], kval[:, 0 if g == 0 else 1, :].bitcast(F32)).then_inc(kv_st, 16)

        def group(g, u, i):
            if runs(g, 0, GROUPS - 4):
                eng.wait_ge(ln1_act, 2 * g + 6)
                plain(eng)
                load_in((2 * g + 6, 2 * g + 7), 1 - u)
            eng.wait_ge(qk_lo, 4 * g + 4)
            plain(eng)
            eng.dma_start(q_scr[g].rearrange("l m j p x -> p (l m j) x"),
                          q_ev[:, :, :, :].rearrange("p l m (j x) -> p (l m j) x", j=2).bitcast(F32)).then_inc(qk_st, 16)
            eng.dma_start(k_scr[g].rearrange("l m p x -> p l m x"), k_ev[:, :, :, :].bitcast(F32)).then_inc(qk_st, 16)
            if isinstance(g, int) and g in (GROUPS - 3, GROUPS - 2):
                eng.wait_ge(pre_pool, 6)
                eng.wait_ge(kv_st, 16 * GROUPS)
                eng.wait_ge(qk_st, 32 * g)
                load_stacked(eng, T, 0, 0, qk0_ld, halves=(g - (GROUPS - 3),))

        for_groups(eng, group)
        eng.wait_ge(qk_st, 32 * GROUPS)
        eng.wait_ge(qk0_ld, LD)
        eng.wait_ge(z_st, 16)

    @block.scalar
    def _(eng):
        for j, w in enumerate(("wq", "wk", "wv", "wo")):
            eng.dma_start(w_raw[:, :, j * D:(j + 1) * D], A[w]).then_inc(w_ld, 16)
        eng.dma_start(wmod[:, :, 2 * D:6 * D], A["wmod"][:, :, 2 * D:6 * D]).then_inc(wm_ld[1], 16)
        eng.dma_start(r_raw[:, :, 0:NE], A["rg"]).then_inc(e_ld, 16)
        eng.dma_start(r_raw[:, :, NE:2 * NE], A["ru"]).then_inc(e_ld, 16)
        eng.dma_start(esc[:, 0, :], A["escale"].partition_broadcast(P)).then_inc(e_ld, 16)
        eng.dma_start(esc[:, 1, :], A["ebias"].partition_broadcast(P)).then_inc(e_ld, 16)
        eng.wait_ge(c_ld, 16)
        eng.activation(c_tmp[:, 0, :], c_in[:, :], ACT.Exp, scale=-1.0).then_inc(c_exp, 1)

        def normalise_x(g, par):
            eng.wait_ge(ln1_dve, L1_OPS * (g + 2))
            if runs(g, 0):
                eng.wait_ge(ln1_mod, g + 1)
            for j in range(2):
                eng.activation(xn[:, j, :], x_in[:, par, j, :], ACT.Identity, bias=ln_nm[:, j:j + 1],
                               scale=ln_rs[:, j:j + 1]).then_inc(ln1_act, 1)

        def h_hi(g, par, tiles):
            eng.wait_ge(th1_mm, g + 2)
            if runs(g, 1):
                eng.wait_ge(carry, g)
            if runs(g, 2):
                eng.wait_ge(v_mm, 2 * g - 2)
            v = TH[par][:, :].rearrange("p (j k c q) -> p j k c q", j=2, k=KD, c=2)
            for j in tiles:
                eng.activation(hT[:, par, :, 0, :, CH * (1 + j):CH * (2 + j)], v[:, j], ACT.Copy).then_inc(hT_hi, 1)

        normalise_x(-1, 1)
        normalise_x(0, 0)
        eng.wait_ge(w_ld, 64)
        eng.activation(w_hl[:, :, 0, :], w_raw[:, :, 0:3 * D], ACT.Copy).then_inc(w_hi, 1)
        h_hi(-1, 1, (1,))
        h_hi(0, 0, (0, 1))
        normalise_x(1, 1)

        def group(g, u, i):
            for j, ev in enumerate((q_ev, q_ev, k_ev, k_ev)):
                if j == 0 and runs(g, 1):
                    eng.wait_ge(qk_st, 32 * g)
                eng.wait_ge(qk_mm, 4 * g + j + 1)
                eng.activation(ev[:, 0, j % 2, :], QB[j][:, 0:ev.shape[3]], ACT.Copy).then_inc(qk_hi, 1)
            if runs(g, 0, GROUPS - 3):
                normalise_x(g + 2, u)
            if runs(g, 0, GROUPS - 2):
                h_hi(g + 1, 1 - u, (0, 1))
            for j in range(2):
                eng.wait_ge(v_mm, 2 * g + j + 1)
                plain(eng)
                eng.activation(VW[:, bass.ds(2 * g + j, 1), :, 0:2 * DH].rearrange("p o h (w d) -> p (o w) h d", w=2),
                               VB[j][:, :].rearrange("p (w h d) -> p w h d", w=2, h=HEADS), ACT.Copy).then_inc(v_ev, 1)
            if isinstance(g, int) and g == GROUPS - 3:
                eng.wait_ge(wo_dve, KD)
                eng.activation(wo_hl[:, :, 0, :], w_raw[:, :, 3 * D:4 * D], ACT.Copy).then_inc(wo_hi, 1)

        for_groups(eng, group)

    @block.gpsimd
    def _(eng):
        eng.memset(kval[:, :, :].bitcast(F32), 0.0).then_inc(pre_pool, 1)
        eng.wait_ge(pre_pool, 1)
        eng.memset(kval[:, 0, 0:CH].bitcast(F32), -BIG).then_inc(pre_pool, 1)
        eng.wait_ge(pre_pool, 2)
        for i in range(2):
            eng.memset(Q2[i][:, :, :, :, :].bitcast(F32), 0.0).then_inc(pre_pool, 1)
        eng.wait_ge(pre_pool, 4)
        for i in range(2):
            eng.memset(Q2[i][VALID:VALID + 1, :, :, :, 0:CH].bitcast(F32), 1.0).then_inc(pre_pool, 1)
        eng.wait_ge(pre_pool, 6)
        eng.memset(T["zeros"][:, :], 0.0).then_inc(z_set, 1)
        eng.wait_ge(z_set, 1)
        eng.dma_start(T["xs_scr"][NE * CAP:NE * CAP + P, :], T["zeros"][:, :]).then_inc(z_st, 16)

        def modulate(g):
            eng.wait_ge(ln1_act, 2 * g + 4)
            if runs(g, 0):
                eng.wait_ge(h1_ready, g + 1)
            eng.tensor_tensor(h_t[:, :, :], xn[:, :, :], mod[:, 1:2, :].broadcast_to([P, 2, D]), ALU.mult).then_inc(ln1_mod, 1)
            eng.wait_ge(ln1_mod, g + 2)
            if runs(g, 0):
                eng.wait_ge(th1_mm, g + 1)
            eng.tensor_tensor(h[:, :, :], h_t[:, :, :], mod[:, 0:1, :].broadcast_to([P, 2, D]), ALU.add).then_inc(h1_ready, 1)

        def carry_on(g, par):
            eng.wait_ge(hT_lo, 2 * g + 1)
            if runs(g, 2):
                eng.wait_ge(v_mm, 2 * g - 2)
            plain(eng)
            a = hT[:, par].rearrange("p k l c x -> p (k l c) x")
            b = hT[:, 1 - par].rearrange("p k l c x -> p (k l c) x")
            last = b[:, :, 2 * CH:3 * CH]
            eng.tensor_scalar(a[:, :, 0:CH], last.bitcast(F32), 1.0, None, ALU.mult).then_inc(carry, 1)

        eng.wait_ge(mod_cp, 2)
        modulate(-1)
        modulate(0)
        carry_on(0, 0)
        modulate(1)

        def group(g, u, i):
            if runs(g, 0, GROUPS - 2):
                carry_on(g + 1, 1 - u)
            if runs(g, 0, GROUPS - 3):
                modulate(g + 2)

        for_groups(eng, group)

    @block.vector
    def _(eng):
        def f(ap):
            return ap.bitcast(F32)

        eng.memset(ones_f[:, :], 1.0).then_inc(c_dve, 1)
        ch = Chain(eng, c_dve, 1)
        eng.wait_ge(c_exp, 1)
        ch.mark(eng.tensor_scalar(c_tmp[:, 1, :], c_tmp[:, 0, :], 1.0, None, ALU.add)).wait()
        ch.mark(eng.reciprocal(c_tmp[:, 2, :], c_tmp[:, 1, :])).wait()
        ch.mark(eng.tensor_tensor(c_tmp[:, 3, :], c_in[:, :], c_tmp[:, 2, :], ALU.mult)).wait()
        for k in range(KD):
            eng.tensor_scalar(c_col[:, k, :], ones_f[:, :], c_tmp[:, 3, k:k + 1], None, ALU.mult).then_inc(c_col_done, 1)

        def stats(g, par, count):
            ch = Chain(eng, ln1_dve, L1_OPS * (g + 1))
            eng.wait_ge(xin_ld[par], 64 * count)
            if runs(g, 0):
                eng.wait_ge(ln1_act, 2 * g + 2)
                ch.wait()
            plain(eng)
            for j in range(2):
                ch.mark(eng.bn_stats(ln_st[:, j, :], x_in[:, par, j, :]))
            ch.wait(True)
            for j in range(2):
                ch.mark(eng.bn_aggr(ln_mv[:, j, :], ln_st[:, j, :]))
            ch.wait()
            inverse_std(eng, ch, ln_mv, ln_nw, ln_rs, ln_nm)
            assert ch.k == L1_OPS

        def h_lo(g, par, tiles):
            v = TH[par][:, :].rearrange("p (j k c q) -> p j k c q", j=2, k=KD, c=2)
            eng.wait_ge(hT_hi, 2 * g + 3)
            for j in tiles:
                eng.tensor_tensor(hT[:, par, :, 1, :, CH * (1 + j):CH * (2 + j)], v[:, j],
                                  f(hT[:, par, :, 0, :, CH * (1 + j):CH * (2 + j)]), ALU.subtract).then_inc(hT_lo, 1)

        stats(-1, 1, 1)
        stats(0, 0, 1)
        eng.wait_ge(mod_mm, 1)
        eng.tensor_scalar(mod[:, 0, :], QB[0][:, 0:D], 1.0, None, ALU.mult).then_inc(mod_cp, 1)
        eng.tensor_scalar(mod[:, 1, :], QB[0][:, D:2 * D], 1.0, None, ALU.add).then_inc(mod_cp, 1)
        eng.wait_ge(w_hi, 1)
        eng.tensor_tensor(w_hl[:, :, 1, :], w_raw[:, :, 0:3 * D], f(w_hl[:, :, 0, :]), ALU.subtract).then_inc(w_lo, 1)
        stats(1, 1, 2)
        h_lo(-1, 1, (1,))
        h_lo(0, 0, (0, 1))
        eng.wait_ge(mod_mm, 3)
        eng.tensor_scalar(mod[:, 2, :], VB[0][:, D:2 * D], 1.0, None, ALU.mult).then_inc(mod_cp, 1)
        eng.tensor_scalar(mod[:, 3, :], VB[1][:, 0:D], 1.0, None, ALU.add).then_inc(mod_cp, 1)
        for i, raw in enumerate((VB[0][:, 0:D], VB[1][:, D:2 * D])):
            ch = Chain(eng, gate_dve, 5 * i)
            if i:
                ch.wait()
            ch.mark(eng.tensor_scalar(g_tmp[:, 2, :], raw, -1.0, 0.25, ALU.mult, ALU.max))
            ch.mark(eng.tensor_scalar(g_tmp[:, 1, :], raw, 0.0, 2.0, ALU.is_ge, ALU.mult)).wait()
            ch.mark(eng.tensor_tensor(g_tmp[:, 0, :], raw, g_tmp[:, 2, :], ALU.max)).wait()
            eng.scalar_tensor_tensor(out=(gate_a[:, :], T["gb"][:, :])[i], in0=g_tmp[:, 1, :], scalar=-1.0,
                                     in1=g_tmp[:, 0, :], op0=ALU.add, op1=ALU.mult).then_inc(gate_dve, 2)

        def constants_and_out_weights():
            eng.wait_ge(gate_dve, 5)
            for k in range(KD):
                eng.tensor_tensor(w_raw[:, k, 3 * D:4 * D], w_raw[:, k, 3 * D:4 * D], gate_a[:, :], ALU.mult).then_inc(wo_dve, 1)
            eng.wait_ge(k_ld, 64)
            eng.tensor_copy(mask_key[:, :], mk_raw[:, 0, :]).then_inc(cst, 1)
            eng.tensor_copy(mask_qry[:, :], mk_raw[0:MASKS, 1, :]).then_inc(cst, 1)
            eng.tensor_copy(tri[:, :, :], tri_raw[:, :, :]).then_inc(cst, 1)
            for i in range(2):
                eng.tensor_copy(MM[i][0:MASKS, :].rearrange("p (h x) -> p h x", h=HEADS),
                                mk_raw[0:MASKS, 1:2, :].broadcast_to([MASKS, HEADS, P])).then_inc(cst, 1)
            eng.memset(VW[:, :, :, ONE_V:VC], 1.0).then_inc(cst, 1)
            eng.wait_ge(e_ld, 64)
            eng.tensor_copy(r_hl[:, :, 0, :], r_raw[:, :, :]).then_inc(cst, 1)
            eng.wait_ge(cst, 7)
            eng.tensor_tensor(r_hl[:, :, 1, :], r_raw[:, :, :], f(r_hl[:, :, 0, :]), ALU.subtract).then_inc(cst, 1)

        def group(g, u, i):
            for j, ev in enumerate((q_ev, q_ev, k_ev, k_ev)):
                eng.wait_ge(qk_hi, 4 * g + j + 1)
                eng.tensor_tensor(ev[:, 1, j % 2, :], QB[j][:, 0:ev.shape[3]], f(ev[:, 0, j % 2, :]), ALU.subtract).then_inc(qk_lo, 1)
            if runs(g, 0, GROUPS - 2):
                h_lo(g + 1, 1 - u, (0, 1))
            if runs(g, 0, GROUPS - 4):
                stats(g + 3, 1 - u, i + 3)
            if isinstance(g, int) and g == 0:
                constants_and_out_weights()
            if isinstance(g, int) and g == GROUPS - 1:
                eng.wait_ge(wo_hi, 1)
                eng.tensor_tensor(wo_hl[:, :, 1, :], w_raw[:, :, 3 * D:4 * D], f(wo_hl[:, :, 0, :]), ALU.subtract).then_inc(wo_lo, 1)

        stats(2, 0, 2)
        for_groups(eng, group)

    @block.tensor
    def _(eng):
        def modulation(b, bank):
            for k in range(KD):
                mm = eng.matmul(bank[:, :], c_col[:, k, :], wmod[:, k, 2 * D * b:2 * D * (b + 1)], start=(k == 0),
                                stop=(k == KD - 1))
            mm.then_inc(mod_mm, 1)

        def transpose_h(g, par, tiles):
            eng.wait_ge(h1_ready, g + 2)
            if runs(g, 1):
                eng.wait_ge(hT_lo, 2 * g - 1)
            for j in tiles:
                for k in range(KD):
                    o = (2 * j + k) * P
                    mm = eng.transpose(TH[par][:, o:o + P], h[:, j, k * P:(k + 1) * P], ident[:, :])
            mm.then_inc(th1_mm, 1)

        eng.wait_ge(c_col_done, 2)
        eng.wait_ge(wm_ld[0], 16)
        modulation(0, QB[0])
        eng.wait_ge(wm_ld[1], 16)
        modulation(1, VB[0])
        modulation(2, VB[1])
        eng.wait_ge(k_ld, 64)
        transpose_h(-1, 1, (1,))
        transpose_h(0, 0, (0, 1))
        eng.wait_ge(w_lo, 1)
        eng.wait_ge(mod_cp, 2)

        def group(g, u, i):
            eng.wait_ge(hT_lo, 2 * g + 3)
            eng.wait_ge(carry, g + 1)
            for j in range(4):
                if runs(g, 1):
                    eng.wait_ge(qk_lo, 4 * g + j - 3)
                cols = slice((j // 2) * D + (j % 2) * P, (j // 2) * D + (j % 2) * P + P)
                if j < 2:
                    dst = QB[j][:, 0:2 * P].rearrange("p (t c x) -> p t c x", t=2, c=2)
                    src = [[hT[:, u, k, hl, :, CH:WIN].rearrange("p c (t x) -> p t c x", t=2) for hl in range(2)] for k in range(KD)]
                else:
                    dst = QB[j][:, 0:2 * WIN]
                    src = [[hT[:, u, k, hl, :, :] for hl in range(2)] for k in range(KD)]
                three(eng, dst, [(w_hl[:, k, 0, cols], w_hl[:, k, 1, cols], *src[k]) for k in range(KD)]).then_inc(qk_mm, 1)
            if runs(g, 0, GROUPS - 2):
                transpose_h(g + 1, 1 - u, (0, 1))
            for j in range(2):
                if runs(g, 1):
                    eng.wait_ge(v_ev, 2 * g + j - 1)
                elif j == 0:
                    eng.wait_ge(mod_cp, 4)
                    eng.wait_ge(gate_dve, 10)
                win = slice(CH * j, CH * (j + 2))
                for c in range(2):
                    mm = three(eng, VB[j][:, c * D:(c + 1) * D],
                               [(hT[:, u, k, 0, c, win], hT[:, u, k, 1, c, win], w_hl[:, k, 0, 2 * D:3 * D], w_hl[:, k, 1, 2 * D:3 * D])
                                for k in range(KD)])
                mm.then_inc(v_mm, 1)

        for_groups(eng, group)


def attention_and_routing(nc, A, T, ctx, own):

    def sb(name, shape, dt=F32):
        return ctx.enter_context(nc.sbuf_tensor(name, shape, dt))

    def pb(name, shape):
        return ctx.enter_context(nc.psum_tensor(name, shape, F32))

    def sem(name):
        return own.enter_context(nc.semaphore(name))

    def sems(name, n):
        return [sem(f"{name}{i}") for i in range(n)]

    ident, iota_e, pack, mod, VW, Q2, K2, MM = [T[x] for x in ("ident", "iota_e", "pack", "mod", "VW", "Q2", "K2", "MM")]
    mask_key, mask_qry, tri, r_hl, esc, wo_hl = [T[x] for x in ("mask_key", "mask_qry", "tri", "r_hl", "esc", "wo_hl")]

    x_res = sb("x_res", [P, 4, D])
    x1 = sb("x1", [P, 4, D])
    ln_st = sb("ln2_st", [P, 6])
    ln_mv = sb("ln2_mv", [P, 1, 2])
    ln_nw = sb("ln2_nw", [P, 4, 1])
    ln_rs = sb("ln2_rs", [P, 1])
    ln_nm = sb("ln2_nm", [P, 1])
    neg_m = sb("neg_m", [P, 2, HEADS])
    mT = sb("mT", [HEADS, 2, P], F32R)
    prob = sb("prob", [P, 4, 4 * P])
    rden = sb("rden", [P, 2, 8])
    o_n = sb("o_n", [P, D])
    oT = sb("oT", [P, 2, KD, P], F32R)
    xn2 = sb("xn2", [P, D])
    h2t = sb("h2t", [P, D])
    h2T = sb("h2T", [P, 4, 2, KD, P], F32R)
    rt = sb("rt", [P, 10, 2, NE])
    r_sm = sb("r_sm", [P, 3, 2])
    top8 = sb("top8", [P, 2, 8])
    top8i = sb("top8i", [P, 2, 8], U32)
    pk = sb("pk", [P, 2, 2, 3 * TOPK])
    onehot = sb("onehot", [P, 2, 2, TOPK, NE])
    ohw = sb("ohw", [P, 2, TOPK, NE])
    ohs = sb("ohs", [P, 2, TOPK, NE])
    rank_f = sb("rank_f", [P, 2, NE])
    mask_e = sb("mask_e", [P, 2, 2, NE], F32R)
    msum = sb("msum", [P, 2, 2, NE], F32R)
    h2, slot_u, disp = T["h2"], T["slot_u"], T["disp"]

    X, Y = pb("X", [P, 512]), pb("Y", [P, 512])
    SB = [pb(f"SB{i}", [P, 512]) for i in range(2)]
    TB = [pb(f"TB{i}", [P, 512]) for i in range(2)]
    O = pb("O", [P, 2, 512])

    first, xres_ld, qk_ld = sem("first"), sems("xres_ld", 4), sem("qk_ld")
    s_mm, s_red, mt_mm, mt_cp = sem("s_mm"), sem("s_red"), sem("mt_mm"), sem("mt_cp")
    mm_ld = sems("mm_ld", 2)
    st_mm, exp_done, pv_mm, nrm = sem("st_mm"), sem("exp_done"), sem("pv_mm"), sem("nrm")
    to_mm, oT_hi, oT_lo, out_mm = sem("to_mm"), sem("oT_hi"), sem("oT_lo"), sem("out_mm")
    ln2_dve, ln2_act, ln2_mod, h2_ready = [sem(x) for x in ("ln2_dve", "ln2_act", "ln2_mod", "h2_ready")]
    th2_mm, h2T_hi, h2T_lo = sem("th2_mm"), sem("h2T_hi"), sem("h2T_lo")
    x1_st, h2_st = sems("x1_st", 4), sems("h2_st", 4)
    r_mm, r_act, r_dve, rank_mm, p_dve = [sem(x) for x in ("r_mm", "r_act", "r_dve", "rank_mm", "p_dve")]
    cnt_mm, cnt_cp = sem("cnt_mm"), sem("cnt_cp")
    block = ctx.enter_context(nc.Block())
    x_t = A["x"].rearrange("(c n q) d -> n c q d", c=2, n=TILES)
    LAST = TILES - 1

    @block.sync
    def _(eng):
        for t in range(4):
            for credit in (x1_st[t], h2_st[t]):
                eng.nop(nofuse=True).then_inc(credit, 16)

        def load_res(n, t):
            if runs(n, 4):
                eng.wait_ge(ln2_dve, L2_OPS * (n - 4) + 1)
                plain(eng)
            for c in range(2):
                eng.dma_start(x_res[c * CH:(c + 1) * CH, t, :], x_t[n, c]).then_inc(xres_ld[t], 16)

        def put_max(n, p2):
            eng.wait_ge(mt_cp, n + 1)
            plain(eng)
            if runs(n, 2):
                eng.wait_ge(st_mm, 4 * n - 4)
            eng.dma_start(MM[p2][MASKS:MASKS + 1, :].bitcast(F32).rearrange("o (h x) -> o h x", h=HEADS),
                          mT[:, p2, :].bitcast(F32)).then_inc(mm_ld[p2], 16)

        def keep_x1(n, t):
            eng.wait_ge(ln2_dve, L2_OPS * n + 1)
            plain(eng)
            eng.dma_start(T["x1_scr"][n], x1[:, t, :]).then_inc(x1_st[t], 16)

        def keep_h2(n, t):
            eng.wait_ge(h2_ready, n + 1)
            plain(eng)
            eng.dma_start(T["h2_scr"][n], h2[:, t, :]).then_inc(h2_st[t], 16)

        put_max(0, 0)

        def tile(n, t, e, i):
            if t % 2 == 0 and runs(n, 0, TILES - 3):
                if runs(n, 2):
                    eng.wait_ge(st_mm, 4 * n)
                    plain(eng)
                load_stacked(eng, T, e + 1, (t // 2 + 1) % 2, qk_ld)
            load_res(n, t)
            if runs(n, 0, TILES - 2):
                put_max(n + 1, (t + 1) % 2)
            if runs(n, 2):
                keep_h2(n - 2, (t - 2) % 4)
            if runs(n, 1):
                keep_x1(n - 1, (t - 1) % 4)
            if isinstance(n, int) and n < 4:
                for x in range(FIRST // 4 * n, FIRST // 4 * (n + 1)):
                    eng.dma_start(T["gu_first"][:, x], A["egu"][:, x]).then_inc(T["w_first"], 16)
                    eng.dma_start(T["dn_first"][:, x], A["ed"][:, x]).then_inc(T["w_first"], 16)

        for_tiles(eng, tile)
        keep_x1(LAST, 3)
        keep_h2(LAST - 1, 2)
        keep_h2(LAST, 3)
        for t in range(4):
            eng.wait_ge(x1_st[t], 16 * (TILES // 4) + 16)
            eng.wait_ge(h2_st[t], 16 * (TILES // 4) + 16)
            if t < 2:
                eng.wait_ge(disp[t], 16 * TOPK * (TILES // 4) + 16)

    @block.scalar
    def _(eng):
        def max_out(n, e, p2):
            eng.wait_ge(mt_mm, n + 1)
            if runs(n, 2):
                eng.wait_ge(mm_ld[p2], 16 * e)
            eng.activation(mT[:, p2, :], Y[0:HEADS, 0:P], ACT.Copy).then_inc(mt_cp, 1)

        def o_hi(m):
            eng.wait_ge(to_mm, m + 1)
            eng.activation(oT[:, 0, :, :], Y[:, 0:D].rearrange("p (k x) -> p k x", k=KD), ACT.Copy).then_inc(oT_hi, 1)

        def normalise_x1(m, tm):
            eng.wait_ge(ln2_dve, L2_OPS * (m + 1))
            if runs(m, 1):
                eng.wait_ge(ln2_mod, m)
            eng.activation(xn2[:, :], x1[:, tm, :], ACT.Identity, bias=ln_nm[:, 0:1],
                           scale=ln_rs[:, 0:1]).then_inc(ln2_act, 1)

        def h2_hi(m, tm):
            eng.wait_ge(th2_mm, m + 1)
            eng.activation(h2T[:, tm, 0, :, :], X[:, 0:D].rearrange("p (k x) -> p k x", k=KD), ACT.Copy).then_inc(h2T_hi, 1)

        def router_exp(g, part):
            if part == 0:
                eng.wait_ge(r_mm, g + 1)
                v = X[:, 0:4 * NE].rearrange("p (a u x) -> p a u x", a=2, u=2)
                if runs(g, 1):
                    eng.wait_ge(r_dve, R_OPS * g)
                eng.activation(rt[:, 0, :, :], v[:, :, 0, :], ACT.Exp, scale=-1.0).then_inc(r_act, 1)
            else:
                eng.wait_ge(r_dve, R_OPS * g + 7)
                eng.activation(rt[:, 6, :, :], rt[:, 5, :, :], ACT.Exp).then_inc(r_act, 1)

        max_out(0, 0, 0)

        def tile(n, t, e, i):
            for q in range(4):
                eng.wait_ge(st_mm, 4 * n + q + 1)
                if runs(n, 1):
                    eng.wait_ge(pv_mm, 4 * n + q - 3)
                eng.activation(prob[:, q, :], TB[q % 2][:, :], ACT.Exp, scale=SCALE).then_inc(exp_done, 1)
                if q == 0 and runs(n, 1):
                    o_hi(n - 1)
                if q == 0 and t % 2 == 0 and runs(n, 4):
                    router_exp(e - 2, 0)
                if q == 2 and runs(n, 0, TILES - 2):
                    max_out(n + 1, e + t % 2, (t + 1) % 2)
                if q == 2 and t % 2 == 0 and runs(n, 4):
                    router_exp(e - 2, 1)
            if runs(n, 2):
                h2_hi(n - 2, (t - 2) % 4)
            if runs(n, 1):
                normalise_x1(n - 1, (t - 1) % 4)

        for_tiles(eng, tile)
        router_exp(GROUPS - 2, 0)
        o_hi(LAST)
        router_exp(GROUPS - 2, 1)
        h2_hi(LAST - 1, 2)
        normalise_x1(LAST, 3)
        h2_hi(LAST, 3)
        router_exp(GROUPS - 1, 0)
        router_exp(GROUPS - 1, 1)

    @block.gpsimd
    def _(eng):
        for t in range(4):
            r = P // 4 * t
            eng.dma_start(T["xs_scr"][NE * CAP + r:NE * CAP + r + P // 4, :],
                          T["zeros"][r:r + P // 4, :]).then_inc(disp[t], 16)

        def modulate(m, tm, im):
            eng.wait_ge(ln2_act, m + 1)
            if runs(m, 1):
                eng.wait_ge(h2_ready, m)
            eng.tensor_tensor(h2t[:, :], xn2[:, :], mod[:, 3, :], ALU.mult).then_inc(ln2_mod, 1)
            eng.wait_ge(ln2_mod, m + 1)
            if runs(m, 4):
                eng.wait_ge(th2_mm, m - 2)
                eng.wait_ge(h2_st[tm], 16 * im + 16)
                eng.wait_ge(disp[tm], 16 * TOPK * im + 16)
            eng.tensor_tensor(h2[:, tm, :], h2t[:, :], mod[:, 2, :], ALU.add).then_inc(h2_ready, 1)

        def dispatch(g, t, par):
            eng.wait_ge(p_dve, P_OPS * g + 4)
            plain(eng)
            send_rows(eng, T, t, par)

        def tile(n, t, e, i):
            if t % 2 == 1 and runs(n, 5):
                dispatch(e - 2, (t - 5) % 4, (t // 2) % 2)
            if runs(n, 1):
                modulate(n - 1, (t - 1) % 4, i if t else i - 1)
            if t % 2 == 1 and runs(n, 5):
                dispatch(e - 2, (t - 4) % 4, (t // 2) % 2)

        for_tiles(eng, tile)
        modulate(LAST, 3, TILES // 4 - 1)
        for j in range(2):
            dispatch(GROUPS - 2, (2 * (GROUPS - 2) + j) % 4, GROUPS % 2)

    @block.vector
    def _(eng):
        def f(ap):
            return ap.bitcast(F32)

        def row_max(n, p2, q):
            eng.wait_ge(s_mm, 4 * n + q + 1)
            if q == 0 and runs(n, 2):
                eng.wait_ge(mt_mm, n - 1)
            eng.tensor_reduce(neg_m[:, p2, 4 * q:4 * q + 4], SB[q % 2][:, :].rearrange("p (h x) -> p h x", h=4),
                              AX.X, ALU.max, negate=True).then_inc(s_red, 1)

        def normalise(m):
            eng.wait_ge(pv_mm, 4 * m + 4)
            if runs(m, 1):
                eng.wait_ge(to_mm, m)
            v = O[:, :, 0:8 * VC].rearrange("p b (h x) -> p b h x", x=VC)
            eng.reciprocal(rden[:, :, :], v[:, :, :, ONE_V]).then_inc(nrm, 1)
            eng.wait_ge(nrm, 3 * m + 1)
            for c in range(2):
                r = slice(c * CH, (c + 1) * CH)
                eng.tensor_tensor(o_n[r, :].rearrange("p (b h d) -> p b h d", b=2, h=8), v[r, :, :, c * DH:(c + 1) * DH],
                                  rden[r, :, :].unsqueeze(3).broadcast_to([CH, 2, 8, DH]), ALU.mult).then_inc(nrm, 1)

        def o_lo(m):
            eng.wait_ge(oT_hi, m + 1)
            eng.tensor_tensor(oT[:, 1, :, :], Y[:, 0:D].rearrange("p (k x) -> p k x", k=KD), f(oT[:, 0, :, :]),
                              ALU.subtract).then_inc(oT_lo, 1)

        def residual(m, tm, im):
            eng.wait_ge(out_mm, m + 1)
            eng.wait_ge(xres_ld[tm], 32 * im + 32)
            if runs(m, 4):
                eng.wait_ge(x1_st[tm], 16 * im + 16)
                eng.wait_ge(ln2_act, m)
            eng.tensor_tensor(x1[:, tm, :], Y[:, 0:D], x_res[:, tm, :], ALU.add).then_inc(ln2_dve, 1)

        def stats(m, tm):
            ch = Chain(eng, ln2_dve, L2_OPS * m + 1)
            if runs(m, 1):
                eng.wait_ge(ln2_act, m)
            ch.wait(True)
            ch.mark(eng.bn_stats(ln_st[:, :], x1[:, tm, :])).wait(True)
            ch.mark(eng.bn_aggr(ln_mv[:, 0, :], ln_st[:, :])).wait()
            inverse_std(eng, ch, ln_mv, ln_nw, ln_rs, ln_nm)
            assert ch.k == L2_OPS - 1

        def h2_lo(m, tm):
            eng.wait_ge(h2T_hi, m + 1)
            eng.tensor_tensor(h2T[:, tm, 1, :, :], X[:, 0:D].rearrange("p (k x) -> p k x", k=KD),
                              f(h2T[:, tm, 0, :, :]), ALU.subtract).then_inc(h2T_lo, 1)

        def b3(ap):
            return ap.unsqueeze(2).broadcast_to([P, 2, NE])

        def route_scores(g):
            c = Chain(eng, r_dve, R_OPS * g)
            v = X[:, 0:4 * NE].rearrange("p (a u x) -> p a u x", a=2, u=2)
            eng.wait_ge(r_act, 2 * g + 1)
            c.mark(eng.tensor_scalar(rt[:, 1, :, :], rt[:, 0, :, :], 1.0, None, ALU.add)).wait()
            c.mark(eng.reciprocal(rt[:, 2, :, :], rt[:, 1, :, :])).wait()
            c.mark(eng.tensor_tensor(rt[:, 3, :, :], v[:, :, 0, :], rt[:, 2, :, :], ALU.mult)).wait()
            c.mark(eng.tensor_tensor(rt[:, 4, :, :], v[:, :, 1, :], rt[:, 3, :, :], ALU.mult)).wait()
            c.mark(eng.scalar_tensor_tensor(out=rt[:, 9, :, :], in0=rt[:, 4, :, :], scalar=-1.0, in1=rt[:, 4, :, :],
                                            op0=ALU.mult, op1=ALU.max)).wait()
            c.mark(eng.tensor_reduce(r_sm[:, 0, :], rt[:, 9, :, :], AX.X, ALU.max, negate=True)).wait()
            c.mark(eng.tensor_tensor(rt[:, 5, :, :], rt[:, 9, :, :], b3(r_sm[:, 0, :]), ALU.add))
            assert c.k == 7

        def route(g, par):
            c = Chain(eng, r_dve, R_OPS * g + 7)
            eng.wait_ge(r_act, 2 * g + 2)
            c.mark(eng.tensor_reduce(r_sm[:, 1, :], rt[:, 6, :, :], AX.X, ALU.add)).wait()
            c.mark(eng.reciprocal(r_sm[:, 2, :], r_sm[:, 1, :])).wait()
            c.mark(eng.tensor_tensor(rt[:, 7, :, :], rt[:, 6, :, :], b3(r_sm[:, 2, :]), ALU.mult)).wait()
            c.mark(eng.tensor_tensor(rt[:, 8, :, :], rt[:, 7, :, :], esc[:, 1:2, :].broadcast_to([P, 2, NE]), ALU.add))
            c.wait(True)
            for a in range(2):
                c.mark(eng.max(top8[:, a, :], rt[:, 8, a, :]))
            c.wait(True)
            for a in range(2):
                c.mark(eng.max_index(top8i[:, a, :], top8[:, a, :], rt[:, 8, a, :]))
            c.wait()
            c.mark(eng.tensor_scalar(pk[:, par, :, 0:TOPK], top8i[:, :, 0:TOPK], 1.0, None, ALU.mult)).wait()
            c.mark(eng.tensor_tensor(onehot[:, par], pk[:, par, :, 0:TOPK].unsqueeze(3).broadcast_to([P, 2, TOPK, NE]),
                                     iota_e[:, 0:1, :].unsqueeze(1).broadcast_to([P, 2, TOPK, NE]), ALU.is_equal))
            c.mark(eng.tensor_tensor(rt[:, 3, :, :], rt[:, 7, :, :], esc[:, 0:1, :].broadcast_to([P, 2, NE]), ALU.mult)).wait()
            c.mark(eng.tensor_scalar(rt[:, 4, :, :], rt[:, 3, :, :], 1.0, None, ALU.add)).wait()
            c.mark(eng.tensor_tensor(ohw[:, :, :, :], onehot[:, par], rt[:, 4, :, :].unsqueeze(2).broadcast_to([P, 2, TOPK, NE]),
                                     ALU.mult)).wait()
            c.mark(eng.tensor_reduce(pk[:, par, :, 2 * TOPK:3 * TOPK], ohw[:, :, :, :], AX.X, ALU.add))
            if runs(g, 1):
                eng.wait_ge(rank_mm, g)
            with nc.allow_low_precision(reason="zeros and ones"):
                c.mark(eng.tensor_reduce(mask_e[:, par], onehot[:, par].rearrange("p a k x -> p a x k"), AX.X, ALU.add)).wait()
            c.mark(eng.tensor_tensor(msum[:, par, 1, :], f(msum[:, par, 0, :]), f(mask_e[:, par, 0, :]), ALU.add)).wait()
            c.mark(eng.tensor_tensor(msum[:, 1 - par, 0, :], f(msum[:, par, 1, :]), f(mask_e[:, par, 1, :]), ALU.add))
            assert c.k == R_OPS - 7

        def place(g, n, par, prev):
            c = Chain(eng, p_dve, P_OPS * g)
            eng.wait_ge(rank_mm, g + 1)
            v = X[:, 0:2 * NE].rearrange("p (a x) -> p a x", a=2)
            c.mark(eng.tensor_tensor(rank_f[:, :, :], v, iota_e[:, 1:2, :].broadcast_to([P, 2, NE]), ALU.add)).wait()
            c.mark(eng.tensor_tensor(ohs[:, :, :, :], onehot[:, par], rank_f[:, :, :].unsqueeze(2).broadcast_to([P, 2, TOPK, NE]),
                                     ALU.mult)).wait()
            c.mark(eng.tensor_reduce(pk[:, par, :, TOPK:2 * TOPK], ohs[:, :, :, :], AX.X, ALU.add)).wait()
            if prev is not None:
                for t, count in prev:
                    eng.wait_ge(disp[t], count + 16)
            c.mark(eng.tensor_copy(slot_u[:, par, :, :], pk[:, par, :, TOPK:2 * TOPK]))
            c.mark(eng.tensor_scalar(pack[:, bass.ds(n, 2), :], pk[:, par], 1.0, None, ALU.mult)).wait()
            assert c.k == P_OPS

        eng.memset(msum[:, 0, 0, :].bitcast(F32), 0.0).then_inc(first, 1)
        for q in range(4):
            row_max(0, 0, q)

        def tile(n, t, e, i):
            m, tm, im, p2 = n - 1, (t - 1) % 4, i if t else i - 1, (t + 1) % 2
            if runs(n, 1):
                normalise(m)
            if runs(n, 0, TILES - 2):
                row_max(n + 1, p2, 0)
            if runs(n, 1):
                o_lo(m)
            if t % 2 == 0 and runs(n, 4):
                route_scores(e - 2)
            if runs(n, 0, TILES - 2):
                row_max(n + 1, p2, 1)
                row_max(n + 1, p2, 2)
            if t % 2 == 1 and runs(n, 5):
                place(e - 2, n - 5, (t // 2) % 2, [(t - 1, 64 * (i - 1)), (t, 64 * (i - 1))] if runs(n, 9) else None)
            if runs(n, 1):
                residual(m, tm, im)
            if runs(n, 0, TILES - 2):
                row_max(n + 1, p2, 3)
            if runs(n, 2):
                h2_lo(n - 2, (t - 2) % 4)
            if runs(n, 1):
                stats(m, tm)
            if t % 2 == 0 and runs(n, 4):
                route(e - 2, (t // 2) % 2)

        for_tiles(eng, tile)
        im = TILES // 4 - 1
        normalise(LAST)
        route_scores(GROUPS - 2)
        o_lo(LAST)
        residual(LAST, 3, im)
        h2_lo(LAST - 1, 2)
        stats(LAST, 3)
        route(GROUPS - 2, 0)
        place(GROUPS - 2, TILES - 4, 0, [(0, 64 * im), (1, 64 * im)])
        h2_lo(LAST, 3)
        route_scores(GROUPS - 1)
        route(GROUPS - 1, 1)
        place(GROUPS - 1, TILES - 2, 1, [(2, 64 * im), (3, 64 * im)])
        eng.wait_ge(cnt_mm, 1)
        eng.tensor_copy(T["count"][:, :], X[:, 0:NE]).then_inc(cnt_cp, 1)

    @block.tensor
    def _(eng):
        def keys(par, head, j):
            return K2[par][:, head, CH * j:CH * (j + 2)]

        def queries(par, head, j):
            return Q2[par][:, head // 8, j, head % 8, :]

        def scores(n, j, par, q):
            if runs(n, 1) or q >= 2:
                eng.wait_ge(s_red, 4 * n + q - 1)
            bank = SB[q % 2]
            eng.matmul(bank[:, :].rearrange("p (h x) -> p h x", h=4), mask_qry[:, :],
                       mask_key[0:MASKS, :].unsqueeze(1).broadcast_to([MASKS, 4, P]), start=True, stop=True)
            for hh in range(4):
                mm = eng.matmul(bank[:, hh * P:(hh + 1) * P], queries(par, 4 * q + hh, j), keys(par, 4 * q + hh, j),
                                start=False, stop=True, skip_group_check=True)
            mm.then_inc(s_mm, 1)

        def scores_t(n, j, par, p2, q):
            if runs(n, 1) or q >= 2:
                eng.wait_ge(exp_done, 4 * n + q - 1)
            bank = TB[q % 2]
            eng.matmul(bank[:, :], mask_key[:, :], MM[p2][:, 4 * P * q:4 * P * (q + 1)], start=True, stop=True)
            for hh in range(4):
                mm = eng.matmul(bank[:, hh * P:(hh + 1) * P], keys(par, 4 * q + hh, j), queries(par, 4 * q + hh, j),
                                start=False, stop=True, skip_group_check=True)
            mm.then_inc(st_mm, 1)

        def weigh(n, q):
            eng.wait_ge(exp_done, 4 * n + q + 1)
            for hh in range(4):
                head = 4 * q + hh
                mm = eng.matmul(O[:, head // 8, (head % 8) * VC:(head % 8 + 1) * VC], prob[:, q, hh * P:(hh + 1) * P],
                                VW[:, bass.ds(n, 1), head, :].rearrange("p o x -> p (o x)"), start=True, stop=True)
            mm.then_inc(pv_mm, 1)

        def transpose_max(n, p2):
            eng.wait_ge(s_red, 4 * n + 4)
            eng.transpose(Y[0:HEADS, 0:P], neg_m[:, p2, :], ident[:, :]).then_inc(mt_mm, 1)

        def transpose_o(m):
            eng.wait_ge(nrm, 3 * m + 3)
            for k in range(KD):
                mm = eng.transpose(Y[:, k * P:(k + 1) * P], o_n[:, k * P:(k + 1) * P], ident[:, :])
            mm.then_inc(to_mm, 1)

        def project_out(m):
            eng.wait_ge(oT_lo, m + 1)
            three(eng, Y[:, 0:D], [(oT[:, 0, k, :], oT[:, 1, k, :], wo_hl[:, k, 0, :], wo_hl[:, k, 1, :])
                                   for k in range(KD)]).then_inc(out_mm, 1)

        def transpose_h2(m, tm):
            eng.wait_ge(h2_ready, m + 1)
            for k in range(KD):
                mm = eng.transpose(X[:, k * P:(k + 1) * P], h2[:, tm, k * P:(k + 1) * P], ident[:, :])
            mm.then_inc(th2_mm, 1)

        def router(g, t0):
            eng.wait_ge(h2T_lo, 2 * g + 2)
            for a in range(2):
                mm = three(eng, X[:, a * 2 * NE:(a + 1) * 2 * NE],
                           [(h2T[:, t0 + a, 0, k, :], h2T[:, t0 + a, 1, k, :], r_hl[:, k, 0, :], r_hl[:, k, 1, :])
                            for k in range(KD)])
            mm.then_inc(r_mm, 1)

        def ranks(g, par):
            eng.wait_ge(r_dve, R_OPS * g + R_OPS)
            for a in range(2):
                eng.matmul(X[:, a * NE:(a + 1) * NE], tri[:, 0, :], mask_e[:, par, a, :], start=True, stop=False)
                mm = eng.matmul(X[:, a * NE:(a + 1) * NE], tri[:, 1, :], msum[:, par, a, :], start=False, stop=True)
            mm.then_inc(rank_mm, 1)

        for q in range(4):
            scores(0, 0, 0, q)
        transpose_max(0, 0)
        scores(1, 1, 0, 0)

        def tile(n, t, e, i):
            j, par, p2, m = t % 2, (t // 2) % 2, t % 2, n - 1
            n1, j1, par1 = n + 1, (t + 1) % 2, ((t + 1) // 2) % 2
            more = runs(n, 0, TILES - 2)
            eng.wait_ge(mm_ld[p2], 16 * e + 16)
            scores_t(n, j, par, p2, 0)
            if more:
                scores(n1, j1, par1, 1)
            if runs(n, 1):
                if more:
                    eng.wait_ge(mt_cp, n + 1)
                transpose_o(m)
            if t % 2 == 1 and runs(n, 5):
                eng.wait_ge(h2T_lo, n - 2)
                ranks(e - 2, par)
            scores_t(n, j, par, p2, 1)
            if more:
                scores(n1, j1, par1, 2)
            weigh(n, 0)
            if runs(n, 1):
                project_out(m)
            scores_t(n, j, par, p2, 2)
            if more:
                scores(n1, j1, par1, 3)
            weigh(n, 1)
            if more:
                if runs(n, 1):
                    eng.wait_ge(ln2_dve, L2_OPS * m + 1)
                transpose_max(n1, (t + 1) % 2)
            if runs(n, 2):
                if t % 2 == 0 and runs(n, 4):
                    eng.wait_ge(r_dve, R_OPS * (e - 2) + 5)
                if t % 2 == 1 and runs(n, 5):
                    eng.wait_ge(p_dve, P_OPS * (e - 2) + 1)
                transpose_h2(n - 2, (t - 2) % 4)
            scores_t(n, j, par, p2, 3)
            weigh(n, 2)
            weigh(n, 3)
            if t % 2 == 1 and runs(n, 3):
                router(e - 1, (t - 3) % 4)
            if runs(n, 0, TILES - 3):
                if t % 2 == 0:
                    eng.wait_ge(qk_ld, LD * (e + 1))
                scores(n + 2, t % 2, ((t + 2) // 2) % 2, 0)

        for_tiles(eng, tile)
        eng.wait_ge(ln2_dve, L2_OPS * (LAST - 1) + 1)
        transpose_o(LAST)
        project_out(LAST)
        eng.wait_ge(r_dve, R_OPS * (GROUPS - 2) + 5)
        transpose_h2(LAST - 1, 2)
        eng.wait_ge(h2T_lo, LAST)
        ranks(GROUPS - 2, 0)
        eng.wait_ge(p_dve, P_OPS * (GROUPS - 2) + 1)
        transpose_h2(LAST, 3)
        router(GROUPS - 1, 2)
        eng.wait_ge(r_dve, R_OPS * (GROUPS - 1) + 5)
        ranks(GROUPS - 1, 1)
        eng.wait_ge(p_dve, P_OPS * (GROUPS - 1) + 1)
        eng.matmul(X[:, 0:NE], tri[:, 1, :], msum[:, 0, 0, :], start=True, stop=True).then_inc(cnt_mm, 1)


def experts_and_output(nc, A, T, out, ctx, own):

    def sb(name, shape, dt=F32):
        return ctx.enter_context(nc.sbuf_tensor(name, shape, dt))

    def pb(name, shape):
        return ctx.enter_context(nc.psum_tensor(name, shape, F32))

    def sem(name):
        return own.enter_context(nc.semaphore(name))

    def sems(name, n):
        return [sem(f"{name}{i}") for i in range(n)]

    ident, iota_e, pack, count, gb = T["ident"], T["iota_e"], T["pack"], T["count"], T["gb"]
    xs, ys = T["xs_scr"], T["ys_scr"]
    NS = STEPS_RUN

    gu_first, dn_first = T["gu_first"], T["dn_first"]
    gu_raw = sb("gu_raw", [P, NE - FIRST, KD, 2 * FI])
    dn_raw = sb("dn_raw", [FH, NE - FIRST, 2, D])
    gu_hl = sb("gu_hl", [P, RING, KD, 2, 2 * FI], F32R)
    dn_hl = sb("dn_hl", [FH, RING, 2, 2, D], F32R)
    sgu_raw = sb("sgu_raw", [P, KD, 2, SH_I])
    sdn_raw = sb("sdn_raw", [FH, 4, D])
    sgu_hl = sb("sgu_hl", [P, KD, 2, 2, SH_I], F32R)
    sdn_hl = sb("sdn_hl", [FH, 4, 2, D], F32R)

    steps_c = sb("steps_c", [P, 1 + 2 * NE])
    tab = sb("tab", [P, 8, NE])
    tab2 = sb("tab2", [P, 2, NE, NE])
    col = sb("col", [P, 8])
    pair = sb("pair", [P, 2])
    pad_i = sb("pad_i", [P, 2, NE], I32)
    step_i = sb("step_i", [1, 2, P], I32)
    g_oh = sb("g_oh", [P, TILES, TOPK, NE])
    g_sh = sb("g_sh", [P, TILES, TOPK])
    g_row = sb("g_row", [P, TILES, TOPK])
    g_idx = sb("g_idx", [P, TILES, TOPK], U32)

    x_st = sb("x_st", [P, 4, D])
    xT = sb("xT", [P, 2, 2, KD, P], F32R)
    g_act = sb("g_act", [P, 2, SH_I])
    h_act = sb("h_act", [P, 2, SH_I])
    aT = sb("aT", [FH, 2, 2, 4, P], F32R)
    y_st = sb("y_st", [P, 4, D])
    x1_in = sb("x1_in", [P, 2, D])
    z_in = sb("z_in", [P, 2, D])
    y_in = sb("y_in", [P, 4, TOPK, D])
    o_st = sb("o_st", [P, 2, D])
    w_now = sb("w_now", [P, 2, TOPK])
    idx_now = sb("idx_now", [P, 4, TOPK], U32)

    XT = [pb(f"XT{i}", [P, 512]) for i in range(2)]
    GU = [pb(f"GU{i}", [P, 512]) for i in range(2)]
    HT = [pb(f"HT{i}", [P, 512]) for i in range(2)]
    YP = [pb(f"YP{i}", [P, 512]) for i in range(2)]

    cst_ld, sh_ld, w_rest = sem("cst_ld"), sem("sh_ld"), sem("w_rest")
    tb, col_mm, step_tab, g_tab = sem("tb"), sem("col_mm"), sem("step_tab"), sem("g_tab")
    pad_st, pad_rest, sh_split = sem("pad_st"), sem("pad_rest"), sem("sh_split")
    first_hi, first_lo, w_split = sem("first_hi"), sem("first_lo"), sem("w_split")
    xs_ld = sems("xs_ld", 4)
    xt_mm, xT_hi2, xT_lo2 = sem("xt_mm"), sem("xT_hi2"), sem("xT_lo2")
    gu_mm, silu, gated = sem("gu_mm"), sem("silu"), sem("gated")
    ht_mm, aT_hi, aT_lo = sem("ht_mm"), sem("aT_hi"), sem("aT_lo")
    y_mm, y_out = sem("y_mm"), sem("y_out")
    ys_st = sems("ys_st", 4)
    x1_ld, y_gt, fin_dve, o_out = sems("x1_ld", 2), sems("y_gt", 4), sem("fin_dve"), sems("o_out", 2)
    w_cp, idx_cp = sem("w_cp"), sem("idx_cp")
    block = ctx.enter_context(nc.Block())


    def write_pads(eng, start, stride, count, signal):
        with eng.Fori(0, count // 4) as i:
            for e in range(4):
                row = eng.value_load(pad_i[0:1, 0, bass.ds(stride * (4 * i + e) + start, 1)], min_val=0, max_val=NE * CAP)
                eng.dma_start(xs[bass.ds(row, P), :], T["zeros"][:, :]).then_inc(signal, 16)

    @block.sync
    def _(eng):
        eng.dma_start(steps_c[:, :], A["steps"]).then_inc(cst_ld, 16)
        for t in range(4):
            eng.nop(nofuse=True).then_inc(ys_st[t], 16)
        eng.wait_ge(tb, TB_PAD)
        write_pads(eng, 0, 2, NE // 4, pad_st)
        eng.wait_ge(step_tab, 1)
        eng.wait_ge(pad_st, 16 * NE // 2)
        for t in (2, 3):
            eng.wait_ge(T["disp"][t], 16 * TOPK * (TILES // 4) + 16)

        def load_x(w, t):
            if runs(w, 4):
                eng.wait_ge(xt_mm, w - 3)
            row = eng.value_load(step_i[0:1, 0, bass.ds(w, 1)], min_val=0, max_val=NE * CAP)
            eng.dma_start(x_st[:, t, :], xs[bass.ds(row, P), :]).then_inc(xs_ld[t], 16)

        def store_y(w, t):
            eng.wait_ge(y_out, w + 1)
            plain(eng)
            eng.dma_start(ys[bass.ds(P * w, P), :], y_st[:, t, :]).then_inc(ys_st[t], 16)

        for t in range(4):
            load_x(t, t)

        def step(w, t, i, first, last):
            if runs(w, 2):
                store_y(w - 2, (t - 2) % 4)
            if isinstance(w, int) and w == 3:
                eng.wait_ge(pad_rest, 16 * NE // 2)
            if runs(w, 0, NS - 5):
                load_x(w + 4, t)
            else:
                load_h2(w + 4 - NS, t)

        def load_h2(n, t):
            eng.wait_ge(xt_mm, NS + n - 3)
            plain(eng)
            eng.dma_start(x_st[:, t, :], T["h2_scr"][n]).then_inc(xs_ld[t], 16)

        for_steps(eng, step, NS)
        store_y(NS - 2, 2)
        store_y(NS - 1, 3)

        def load_x1(n, t):
            if runs(n, 2):
                eng.wait_ge(fin_dve, FIN * (n - 2) + 1)
                plain(eng)
            eng.dma_start(x1_in[:, t % 2, :], T["x1_scr"][n]).then_inc(x1_ld[t % 2], 16)

        def store_out(n, t):
            eng.wait_ge(fin_dve, FIN * (n + 1))
            plain(eng)
            for c in range(2):
                eng.dma_start(out.rearrange("(c n q) d -> n c q d", c=2, n=TILES)[n, c],
                              o_st[c * CH:(c + 1) * CH, t % 2, :]).then_inc(o_out[t % 2], 16)

        def tile(n, t, e, i):
            if runs(n, 0, TILES - 5):
                load_h2(n + 4, t)
            load_x1(n, t)
            if runs(n, 2):
                store_out(n - 2, (t - 2) % 4)

        for_tiles(eng, tile)
        store_out(TILES - 2, 2)
        store_out(TILES - 1, 3)
        for t in range(2):
            eng.wait_ge(o_out[t], 32 * (TILES // 2))
        for t in range(4):
            eng.wait_ge(ys_st[t], 16 * (NS // 4) + 16)
        eng.wait_ge(pad_st, 16 * NE // 2)
        eng.wait_ge(pad_rest, 16 * NE // 2)

    @block.scalar
    def _(eng):
        def load_rest(into, source, q):
            into_q, from_q = slice(RING * q, RING * (q + 1)), slice(FIRST + RING * q, FIRST + RING * (q + 1))
            eng.dma_start(into[:, into_q], source[:, from_q]).then_inc(w_rest, 16)

        load_rest(gu_raw, A["egu"], 0)

        def x_hi(w, p2):
            eng.wait_ge(xt_mm, w + 1)
            if runs(w, 2):
                eng.wait_ge(gu_mm, w - 1)
            eng.activation(xT[:, p2, 0, :, :], XT[p2][:, 0:D].rearrange("p (k x) -> p k x", k=KD), ACT.Copy).then_inc(xT_hi2, 1)

        def a_hi(w, p2, k):
            eng.wait_ge(ht_mm, w + 1)
            eng.activation(aT[:, p2, 0, 0:k, :], HT[p2][0:FH, 0:k * P].rearrange("p (k x) -> p k x", k=k), ACT.Copy).then_inc(aT_hi, 1)

        for r in range(RING):
            eng.wait_ge(T["w_first"], 32 * FIRST)
            eng.activation(gu_hl[:, r, :, 0, :], gu_first[:, r], ACT.Copy).then_inc(first_hi, 1)
            eng.activation(dn_hl[:, r, :, 0, :], dn_first[:, r], ACT.Copy).then_inc(first_hi, 1)
        eng.wait_ge(tb, TB_PAD)
        write_pads(eng, 1, 2, NE // 4, pad_st)
        x_hi(0, 0)
        x_hi(1, 1)

        def step(w, t, i, first, last):
            p2 = t % 2
            eng.wait_ge(gu_mm, w + 1)
            if runs(w, 2):
                eng.wait_ge(gated, w - 1)
            eng.activation(g_act[:, p2, 0:FI], GU[p2][:, 0:FI], ACT.Silu).then_inc(silu, 1)
            x_hi(w + 2, p2)
            if runs(w, 1):
                if runs(w, 3):
                    eng.wait_ge(y_mm, w - 2)
                a_hi(w - 1, 1 - p2, 2)
            if isinstance(w, int) and w < 3:
                load_rest(*((dn_raw, A["ed"], 0), (gu_raw, A["egu"], 1), (dn_raw, A["ed"], 1))[w])
            if isinstance(w, int) and w == 3:
                eng.dma_start(sgu_raw[:, :, :, :], A["sgu"]).then_inc(sh_ld, 16)
                eng.dma_start(sdn_raw[:, :, :], A["sd"]).then_inc(sh_ld, 16)

        for_steps(eng, step, NS)

        def tile(n, t, e, i):
            w, p2 = NS + n, t % 2
            eng.wait_ge(gu_mm, w + 1)
            eng.wait_ge(gated, w - 1)
            eng.activation(g_act[:, p2, :], GU[0][:, 0:SH_I], ACT.Silu).then_inc(silu, 1)
            if runs(n, 0, TILES - 3):
                x_hi(w + 2, p2)
            eng.wait_ge(y_mm, w - 2)
            a_hi(w - 1, 1 - p2, 4 if runs(n, 1) else 2)

        for_tiles(eng, tile)
        eng.wait_ge(y_mm, NS + TILES - 2)
        a_hi(NS + TILES - 1, 1, 4)

    @block.gpsimd
    def _(eng):
        def split_lo(e, r, raw_g, raw_d):
            eng.tensor_tensor(gu_hl[:, r, :, 1, :], raw_g, gu_hl[:, r, :, 0, :].bitcast(F32), ALU.subtract).then_inc(w_split, 1)
            eng.tensor_tensor(dn_hl[:, r, :, 1, :], raw_d, dn_hl[:, r, :, 0, :].bitcast(F32), ALU.subtract).then_inc(w_split, 1)

        def expert(e, r, raw_g, raw_d):
            zero = T["zeros"][:, 0:1].unsqueeze(2)
            eng.tensor_tensor(gu_hl[:, r, :, 0, :], raw_g, zero.broadcast_to([P, KD, 2 * FI]), ALU.add).then_inc(w_split, 1)
            eng.tensor_tensor(dn_hl[:, r, :, 0, :], raw_d, zero[0:FH].broadcast_to([FH, 2, D]), ALU.add).then_inc(w_split, 1)
            eng.wait_ge(w_split, 4 * (e - RING) + 3)
            if not isinstance(e, int):
                plain(eng)
            split_lo(e, r, raw_g, raw_d)

        for t in (2, 3):
            send_rows(eng, T, t, (GROUPS - 1) % 2)
        eng.nop(nofuse=True).then_inc(w_split, 1)
        eng.wait_ge(tb, TB_PAD)
        write_pads(eng, NE // 2, 1, NE // 2, pad_rest)


        def expert_rings(low, high, raw_g, raw_d, base):
            with eng.Fori(low, high) as i:
                for r in range(RING):
                    e = RING * i + r
                    last = eng.value_load(pad_i[0:1, 1, bass.ds(e - RING, 1)], min_val=0, max_val=NS)
                    eng.wait_ge(y_mm, last)
                    plain(eng)
                    expert(e, r, raw_g[:, bass.ds(e - base, 1)].rearrange("p e k x -> p (e k) x"),
                           raw_d[:, bass.ds(e - base, 1)].rearrange("p e k x -> p (e k) x"))

        eng.wait_ge(T["w_first"], 32 * FIRST)
        expert_rings(1, FIRST // RING, gu_first, dn_first, 0)
        eng.wait_ge(w_rest, 32 * (NE - FIRST) // RING)
        expert_rings(FIRST // RING, NE // RING, gu_raw, dn_raw, FIRST)

        eng.wait_ge(sh_ld, 32)
        c2 = Chain(eng, sh_split, 0)
        c2.mark(eng.tensor_copy(sgu_hl[:, :, 0, :, :], sgu_raw[:, :, :, :]))
        c2.mark(eng.tensor_tensor(sdn_raw[:, :, :], sdn_raw[:, :, :], gb[0:FH, :].unsqueeze(1).broadcast_to([FH, 4, D]),
                                  ALU.mult)).wait()
        c2.mark(eng.tensor_copy(sdn_hl[:, :, 0, :], sdn_raw[:, :, :]))
        c2.mark(eng.tensor_tensor(sgu_hl[:, :, 1, :, :], sgu_raw[:, :, :, :], sgu_hl[:, :, 0, :, :].bitcast(F32),
                                  ALU.subtract)).wait()
        c2.mark(eng.tensor_tensor(sdn_hl[:, :, 1, :], sdn_raw[:, :, :], sdn_hl[:, :, 0, :].bitcast(F32), ALU.subtract))
        assert c2.k == SH_OPS

        eng.wait_ge(g_tab, 1)
        for t in range(4):
            eng.wait_ge(ys_st[t], 16 * (NS // 4) + 16)

        def tile(n, t, e, i):
            if runs(n, 4):
                eng.wait_ge(fin_dve, FIN * (n - 3))
            plain(eng)
            eng.tensor_copy(idx_now[:, t, :], g_idx[:, bass.ds(n, 1), :].rearrange("p o k -> p (o k)")).then_inc(idx_cp, 1)
            eng.wait_ge(idx_cp, n + 1)
            plain(eng)
            for k in range(TOPK):
                eng.indirect_dma_start(y_in[:, t, k, :], None, ys,
                                       bass.IndirectOffsetOnAxis(ap=idx_now[:, t, k:k + 1], axis=0)).then_inc(y_gt[t], 16)

        for_tiles(eng, tile)

    @block.vector
    def _(eng):
        c = Chain(eng, tb, 0)

        def row(i):
            return tab[:, i, :]

        n_t, cum, before, shift, pads = row(0), row(1), row(2), row(3), row(4)
        eng.wait_ge(cst_ld, 16)
        j128, ringw, part = steps_c[:, 1:1 + NE], steps_c[:, 1 + NE:1 + 2 * NE], steps_c[:, 0:1]
        e_row, e_cap = iota_e[:, 0, :], iota_e[:, 1, :]

        def over(ap, outer):
            return (ap.unsqueeze(2) if outer else ap.unsqueeze(1)).broadcast_to([P, NE, NE])

        c.mark(eng.tensor_tensor(tab2[:, 0], over(count[:, :], True), over(j128, False), ALU.is_gt)).wait()
        c.mark(eng.tensor_reduce(row(5), tab2[:, 0], AX.X, ALU.add)).wait()
        c.mark(eng.tensor_scalar(n_t, row(5), 1.0, None, ALU.max))
        c.mark(eng.tensor_tensor(tab2[:, 1], over(e_row, False), over(e_row, True), ALU.is_le)).wait()
        c.mark(eng.tensor_tensor(tab2[:, 0], tab2[:, 1], over(n_t, False), ALU.mult)).wait()
        c.mark(eng.tensor_reduce(cum, tab2[:, 0], AX.X, ALU.add)).wait()
        c.mark(eng.tensor_tensor(before, cum, n_t, ALU.subtract))
        c.mark(eng.tensor_tensor(pads, e_cap, count[:, :], ALU.add)).wait()
        c.mark(eng.tensor_copy(pad_i[:, 0, :], pads))
        c.mark(eng.tensor_copy(pad_i[:, 1, :], cum))
        assert c.k == TB_PAD
        c.mark(eng.scalar_tensor_tensor(out=shift, in0=before, scalar=-float(P), in1=e_cap, op0=ALU.mult, op1=ALU.add))
        c.mark(eng.tensor_scalar(row(5), cum, part, None, ALU.is_le)).wait()
        c.mark(eng.tensor_reduce(col[:, 0:1], row(5), AX.X, ALU.add))
        c.mark(eng.tensor_tensor(row(6), row(5), ringw, ALU.mult)).wait()
        c.mark(eng.tensor_reduce(col[:, 2:3], row(6), AX.X, ALU.add))
        c.mark(eng.tensor_scalar(row(7), e_row, col[:, 0:1], None, ALU.is_equal)).wait()
        c.mark(eng.tensor_tensor(row(6), row(7), shift, ALU.mult)).wait()
        c.mark(eng.tensor_reduce(col[:, 4:5], row(6), AX.X, ALU.add)).wait()
        c.mark(eng.scalar_tensor_tensor(out=col[:, 5:6], in0=part, scalar=float(P), in1=col[:, 4:5], op0=ALU.mult, op1=ALU.add))
        c.mark(eng.tensor_scalar(col[:, 6:7], col[:, 0:1], float(NE), float(NE * CAP), ALU.is_ge, ALU.mult)).wait()
        c.mark(eng.tensor_tensor(col[:, 7:8], col[:, 5:6], col[:, 6:7], ALU.add)).wait()
        c.mark(eng.tensor_scalar(pair[:, 0:1], col[:, 7:8], float(NE * CAP), None, ALU.min))
        c.mark(eng.tensor_scalar(col[:, 3:4], col[:, 0:1], float(1 - RING), 0.0, ALU.add, ALU.max)).wait()
        c.mark(eng.tensor_scalar(col[:, 1:2], col[:, 3:4], float(NE - RING), 4.0, ALU.min, ALU.mult)).wait()
        c.mark(eng.tensor_tensor(pair[:, 1:2], col[:, 1:2], col[:, 2:3], ALU.add))
        assert c.k == TB_COL
        eng.wait_ge(col_mm, 1)
        eng.tensor_copy(step_i[:, :, :], YP[0][0:1, 0:2 * P].rearrange("p (a x) -> p a x", a=2)).then_inc(step_tab, 1)
        for r in range(RING):
            eng.wait_ge(first_hi, 2 * r + 2)
            eng.tensor_tensor(gu_hl[:, r, :, 1, :], gu_first[:, r], gu_hl[:, r, :, 0, :].bitcast(F32), ALU.subtract).then_inc(first_lo, 1)
            eng.tensor_tensor(dn_hl[:, r, :, 1, :], dn_first[:, r], dn_hl[:, r, :, 0, :].bitcast(F32), ALU.subtract).then_inc(first_lo, 1)

        def gather_rows():
            c.mark(eng.tensor_tensor(g_oh[:, :, :, :], pack[:, :, 0:TOPK].unsqueeze(3).broadcast_to([P, TILES, TOPK, NE]),
                                     e_row.unsqueeze(1).unsqueeze(1).broadcast_to([P, TILES, TOPK, NE]), ALU.is_equal)).wait()
            c.mark(eng.tensor_tensor(g_oh[:, :, :, :], g_oh[:, :, :, :],
                                     shift.unsqueeze(1).unsqueeze(1).broadcast_to([P, TILES, TOPK, NE]), ALU.mult)).wait()
            c.mark(eng.tensor_reduce(g_sh[:, :, :], g_oh[:, :, :, :], AX.X, ALU.add)).wait()
            c.mark(eng.tensor_tensor(g_row[:, :, :], pack[:, :, TOPK:2 * TOPK], g_sh[:, :, :], ALU.subtract)).wait()
            eng.tensor_copy(g_idx[:, :, :], g_row[:, :, :]).then_inc(g_tab, 1)

        def x_lo(w, p2):
            eng.wait_ge(xT_hi2, w + 1)
            eng.tensor_tensor(xT[:, p2, 1, :, :], XT[p2][:, 0:D].rearrange("p (k x) -> p k x", k=KD),
                              xT[:, p2, 0, :, :].bitcast(F32), ALU.subtract).then_inc(xT_lo2, 1)

        def a_lo(w, p2, k):
            eng.wait_ge(aT_hi, w + 1)
            eng.tensor_tensor(aT[:, p2, 1, 0:k, :], HT[p2][0:FH, 0:k * P].rearrange("p (k x) -> p k x", k=k),
                              aT[:, p2, 0, 0:k, :].bitcast(F32), ALU.subtract).then_inc(aT_lo, 1)

        def y_gate(w, t, i):
            eng.wait_ge(y_mm, w + 1)
            if runs(w, 4):
                eng.wait_ge(ys_st[t], 16 * i + 16)
            eng.tensor_tensor(y_st[:, t, :], YP[t % 2][:, 0:D], gb[:, :], ALU.mult).then_inc(y_out, 1)

        x_lo(0, 0)
        x_lo(1, 1)
        gather_rows()

        def step(w, t, i, first, last):
            p2 = t % 2
            eng.wait_ge(silu, w + 1)
            if runs(w, 2):
                eng.wait_ge(ht_mm, w - 1)
            eng.tensor_tensor(h_act[:, p2, 0:FI], GU[p2][:, FI:2 * FI], g_act[:, p2, 0:FI], ALU.mult).then_inc(gated, 1)
            x_lo(w + 2, p2)
            if runs(w, 2):
                y_gate(w - 2, (t - 2) % 4, i if t >= 2 else i - 1)
            if runs(w, 1):
                a_lo(w - 1, 1 - p2, 2)

        for_steps(eng, step, NS)
        def finish(n, t, i2, i4):
            p2 = t % 2
            c = Chain(eng, fin_dve, FIN * n)
            eng.wait_ge(y_mm, NS + n + 1)
            eng.wait_ge(x1_ld[p2], 16 * i2 + 16)
            c.mark(eng.tensor_tensor(z_in[:, p2, :], YP[p2][:, 0:D], x1_in[:, p2, :], ALU.add)).wait()
            eng.wait_ge(y_gt[t], 16 * TOPK * (i4 + 1))
            acc = z_in[:, p2, :]
            for k in range(TOPK):
                if k == TOPK - 1 and runs(n, 2):
                    eng.wait_ge(o_out[p2], 32 * i2)
                to = o_st[:, p2, :] if k == TOPK - 1 else z_in[:, p2, :]
                c.mark(eng.scalar_tensor_tensor(out=to, in0=y_in[:, t, k, :], scalar=w_now[:, p2, k:k + 1],
                                                in1=acc, op0=ALU.mult, op1=ALU.add))
                if k < TOPK - 1:
                    c.wait()
            assert c.k == FIN

        def weights(n, p2):
            eng.tensor_scalar(w_now[:, p2, :], pack[:, bass.ds(n, 1), 2 * TOPK:3 * TOPK].rearrange("p o k -> p (o k)"), 1.0,
                              None, ALU.mult).then_inc(w_cp, 1)

        def finish_tile(m, t, i2, i4):
            weights(m, t % 2)
            eng.wait_ge(w_cp, m + 1)
            finish(m, t, i2, i4)

        def tile(n, t, e, i):
            w, p2 = NS + n, t % 2
            eng.wait_ge(silu, w + 1)
            eng.wait_ge(ht_mm, w - 1)
            eng.tensor_tensor(h_act[:, p2, :], GU[1][:, 0:SH_I], g_act[:, p2, :], ALU.mult).then_inc(gated, 1)
            if runs(n, 0, TILES - 3):
                x_lo(w + 2, p2)
            if isinstance(n, int) and n < 2:
                y_gate(w - 2, (t - 2) % 4, NS // 4 - 1)
            if runs(n, 3):
                finish_tile(n - 3, (t - 3) % 4, (4 * i + t - 3) // 2 if isinstance(i, int) else 2 * i + (t - 3) // 2,
                            i if t == 3 else i - 1)
            a_lo(w - 1, 1 - p2, 4 if runs(n, 1) else 2)

        for_tiles(eng, tile)
        a_lo(NS + TILES - 1, 1, 4)
        for n in (TILES - 3, TILES - 2, TILES - 1):
            finish_tile(n, n % 4, n // 2, n // 4)

    @block.tensor
    def _(eng):
        eng.wait_ge(tb, TB_COL)
        for a in range(2):
            mm = eng.matmul(YP[0][0:1, a * P:(a + 1) * P], pair[:, a:a + 1], ident[:, :], start=True, stop=True)
        mm.then_inc(col_mm, 1)
        eng.wait_ge(step_tab, 1)

        def transpose_x(w, t, count):
            eng.wait_ge(xs_ld[t], 16 * count)
            if runs(w, 2):
                eng.wait_ge(xT_lo2, w - 1)
            for k in range(KD):
                mm = eng.transpose(XT[t % 2][:, k * P:(k + 1) * P], x_st[:, t, k * P:(k + 1) * P], ident[:, :])
            mm.then_inc(xt_mm, 1)

        def x_pairs(p2, k):
            return xT[:, p2, 0, k, :], xT[:, p2, 1, k, :]

        def gate_up(w, t, entry):
            (need, slot), p2 = entry, t % 2
            eng.wait_ge(w_split, need + 1)
            eng.wait_ge(xT_lo2, w + 1)
            if runs(w, 2):
                eng.wait_ge(gated, w - 1)
            three(eng, GU[p2][:, 0:2 * FI],
                  [x_pairs(p2, k) + tuple(gu_hl[:, bass.ds(slot, 1), k, hl, :].rearrange("p o x -> p (o x)") for hl in range(2))
                   for k in range(KD)]).then_inc(gu_mm, 1)

        def transpose_a(w, t, tiles):
            p2 = t % 2
            eng.wait_ge(gated, w + 1)
            if runs(w, 2):
                eng.wait_ge(aT_lo, w - 1)
            for k in range(tiles):
                mm = eng.transpose(HT[p2][0:FH, k * P:(k + 1) * P], h_act[:, p2, k * FH:(k + 1) * FH], ident[:, :])
            mm.then_inc(ht_mm, 1)

        def down(w, t, entry):
            slot, p2 = entry[1], t % 2
            eng.wait_ge(aT_lo, w + 1)
            if runs(w, 2):
                eng.wait_ge(y_out, w - 1)
            three(eng, YP[p2][:, 0:D],
                  [(aT[:, p2, 0, k, :], aT[:, p2, 1, k, :]) +
                   tuple(dn_hl[:, bass.ds(slot, 1), k, hl, :].rearrange("p o x -> p (o x)") for hl in range(2))
                   for k in range(2)]).then_inc(y_mm, 1)

        def load_entry(w):
            v = eng.value_load(step_i[0:1, 1, bass.ds(w, 1)], min_val=0, max_val=4 * (NE - RING) + RING - 1)
            return v // 4 * 4, v % 4

        transpose_x(0, 0, 1)
        transpose_x(1, 1, 1)
        eng.wait_ge(first_lo, 2 * RING)
        entry = {}

        def step(w, t, i, first, last):
            if first:
                entry.clear()
                entry[0] = load_entry(w)
            k = len(entry) - 1
            gate_up(w, t, entry[k])
            before = entry[k - 2] if k >= 2 else load_entry(w - 2) if runs(w, 2) else None
            if not last:
                entry[k + 1] = load_entry(w + 1)
            transpose_x(w + 2, (t + 2) % 4, (i + 1) + (1 if t >= 2 else 0))
            if runs(w, 2):
                down(w - 2, (t - 2) % 4, before)
            if runs(w, 1):
                transpose_a(w - 1, (t - 1) % 4, 2)

        for_steps(eng, step, NS)
        eng.wait_ge(sh_split, SH_OPS)

        def shared_down(n, t):
            w, p2 = NS + n, t % 2
            eng.wait_ge(aT_lo, w + 1)
            if runs(n, 2):
                eng.wait_ge(fin_dve, FIN * (n - 2) + 1)
            else:
                eng.wait_ge(y_out, w - 1)
            three(eng, YP[p2][:, 0:D], [(aT[:, p2, 0, k, :], aT[:, p2, 1, k, :], sdn_hl[:, k, 0, :], sdn_hl[:, k, 1, :])
                                        for k in range(4)]).then_inc(y_mm, 1)

        def tile(n, t, e, i):
            w, p2 = NS + n, t % 2
            eng.wait_ge(xT_lo2, w + 1)
            eng.wait_ge(gated, w)
            for u in range(2):
                mm = three(eng, GU[u][:, 0:SH_I], [x_pairs(p2, k) + (sgu_hl[:, k, 0, u, :], sgu_hl[:, k, 1, u, :]) for k in range(KD)])
            mm.then_inc(gu_mm, 1)
            if runs(n, 0, TILES - 3):
                transpose_x(w + 2, (t + 2) % 4, NS // 4 + (i + 1) + (1 if t >= 2 else 0))
            if runs(n, 2):
                shared_down(n - 2, (t - 2) % 4)
            else:
                down(w - 2, (t - 2) % 4, load_entry(w - 2))
            transpose_a(w - 1, (t - 1) % 4, 4 if runs(n, 1) else 2)

        for_tiles(eng, tile)
        transpose_a(NS + TILES - 1, 3, 4)
        shared_down(TILES - 2, 2)
        shared_down(TILES - 1, 3)


def program(nc, A, out):
    with ExitStack() as keep:
        T = {}
        for name, shape in (("q_scr", (GROUPS, 2, 2, 2, P, P)), ("k_scr", (GROUPS, 2, 2, P, 2 * WIN)),
                            ("kv_scr", (GROUPS, HEADS, WIN)), ("x1_scr", (TILES, P, D)), ("h2_scr", (TILES, P, D)),
                            ("xs_scr", (NE * CAP + P, D)), ("ys_scr", (STEPS_RUN * P, D))):
            T[name] = nc.dram_tensor(name, shape, F32).ap()
        for name, shape in (("ident", [P, P]), ("iota_e", [P, 2, NE]), ("gb", [P, D]), ("pack", [P, TILES, 3 * TOPK]),
                            ("count", [P, NE]), ("zeros", [P, D]), ("h2", [P, 4, D])):
            T[name] = keep.enter_context(nc.sbuf_tensor(name, shape, F32))
        T["slot_u"] = keep.enter_context(nc.sbuf_tensor("slot_u", [P, 2, 2, TOPK], U32))
        T["disp"] = [keep.enter_context(nc.semaphore(f"disp{t}")) for t in range(4)]
        lent = keep.enter_context(nc.sbuf_tensor("lent", [P, FIRST * (W_GU + W_DN)], F32))
        T["w_first"] = keep.enter_context(nc.semaphore("w_first"))
        T["lent"] = lent
        T["gu_first"] = lent[:, 0:FIRST * W_GU].rearrange("p (e k x) -> p e k x", e=FIRST, k=KD)
        T["dn_first"] = lent[0:FH, FIRST * W_GU:FIRST * (W_GU + W_DN)].rearrange("p (e k x) -> p e k x", e=FIRST, k=2)
        with ExitStack() as shared:
            for name, shape, dt in (("mod", [P, 4, D], F32), ("VW", [P, TILES, HEADS, VC], F32), ("esc", [P, 2, NE], F32),
                                    ("mask_key", [MASKS + 1, P], F32R), ("mask_qry", [MASKS, P], F32R),
                                    ("tri", [P, 2, P], F32R), ("r_hl", [P, KD, 2, 2 * NE], F32R),
                                    ("wo_hl", [P, KD, 2, D], F32R)):
                T[name] = shared.enter_context(nc.sbuf_tensor(name, shape, dt))
            for name, shape in (("Q2", [VALID + 1, 2, 2, HEADS // 2, P]), ("K2", [VALID + 1, HEADS, WIN]),
                                ("MM", [MASKS + 1, HEADS * P])):
                T[name] = [shared.enter_context(nc.sbuf_tensor(f"{name}_{i}", shape, F32R)) for i in range(2)]
            with ExitStack() as ctx:
                project_qkv(nc, A, T, ctx, keep)
            with ExitStack() as ctx:
                attention_and_routing(nc, A, T, ctx, keep)
        with ExitStack() as ctx:
            experts_and_output(nc, A, T, out, ctx, keep)


def constants():
    import numpy as np

    q, r = np.arange(CH), np.arange(CH - 1)
    masks = np.zeros((MASKS + 1, 2, P), np.float32)
    masks[r, 0, r] = 1
    masks[CH - 1 + r, 0, CH + 1 + r] = 1
    masks[MASKS, 0, :] = 1
    hidden = np.concatenate([q[None, :] > r[:, None], q[None, :] <= r[:, None]], 0)
    masks[:MASKS, 1, :] = np.where(np.concatenate([hidden, hidden], 1), -BIG, 0.0)
    tris = np.zeros((P, 2, P), np.float32)
    tris[:, 0, :] = np.triu(np.ones((P, P)), 1)
    tris[:, 1, :] = 1
    e = np.arange(NE, dtype=np.float32)
    iotas = np.broadcast_to(np.stack([e, e * CAP]), (P, 2, NE))
    ring = np.where(np.arange(NE) % RING == RING - 1, 1 - RING, 1)
    steps = np.concatenate([np.arange(P)[:, None], np.tile(P * e, (P, 1)), np.tile(ring, (P, 1))], 1)
    return {"steps": steps.astype(np.float32), "ident": np.eye(P, dtype=np.float32), "masks": masks, "tris": tris,
            "iotas": np.ascontiguousarray(iotas, dtype=np.float32)}


def host_layout(x):
    import numpy as np

    def cols(w, kp):
        w = np.asarray(w)
        return np.ascontiguousarray(w.T.reshape(-1, kp, w.shape[0]).transpose(1, 0, 2))

    g = {k.replace("L0_ffn_", "").replace("L0_attn_", "").replace("L0_", ""): np.asarray(v) for k, v in x.items()}
    w = g["w_qkv"]
    a = {"x": g["x"][0], "c": np.ascontiguousarray(g["c"].reshape(KD, P).T),
         "wmod": np.ascontiguousarray(g["wmod"].reshape(KD, P, 6 * D).transpose(1, 0, 2)),
         "wq": cols(w[0:D], P), "wk": cols(w[D:2 * D], P), "wv": cols(w[2 * D:], P), "wo": cols(g["w_out"], P),
         "rg": cols(g["rg_w"], P), "ru": cols(g["ru_w"], P), "escale": g["extra_scale"], "ebias": g["extra_bias"],
         "egu": np.ascontiguousarray(np.concatenate([g["Wg"], g["Wu"]], 1).reshape(NE, 2 * FI, KD, P).transpose(3, 0, 2, 1)),
         "ed": np.ascontiguousarray(g["Wd"].reshape(NE, D, 2, FH).transpose(3, 0, 2, 1)),
         "sgu": np.ascontiguousarray(np.stack([g["Sg"], g["Su"]]).reshape(2, SH_I, KD, P).transpose(3, 2, 0, 1)),
         "sd": cols(g["Sd"], FH)}
    return a | constants()


def kernel(**inputs):
    import numpy as np
    import concourse.bacc as bacc
    from concourse.bass_utils import run_bass_kernel_spmd

    nc = bacc.Bacc("TRN2", target_bir_lowering=False, num_devices=1)
    arrays = {f"in_{name}": a for name, a in host_layout(inputs).items()}
    A = {name[3:]: nc.dram_tensor(name, a.shape, mybir.dt.from_np(a.dtype), kind="ExternalInput").ap()
         for name, a in arrays.items()}
    out = nc.dram_tensor("out_x", (S_LEN, D), F32, kind="ExternalOutput").ap()
    program(nc, A, out)
    result = run_bass_kernel_spmd(nc, [arrays], core_ids=[0])
    return np.asarray(result.results[0]["out_x"]).reshape(1, S_LEN, D)
```
